# Optimizing a Trainium2 kernel written in Bass

```python
import numpy as np
import jax
import jax.numpy as jnp

def _softmax(x, axis=-1):
    return jax.nn.softmax(x, axis=axis)

def _gelu(x):
    return jax.nn.gelu(x, approximate=True)

def _silu(x):
    return jax.nn.silu(x)

def _sigmoid(x):
    return jax.nn.sigmoid(x)

def _layernorm(x, axis=-1, eps=1e-05):
    m = jnp.mean(x, axis=axis, keepdims=True)
    v = jnp.var(x, axis=axis, keepdims=True)
    return (x - m) / jnp.sqrt(v + eps)

def _scatter_add(tgt, idx, src, axis=0):
    return tgt.at[idx].add(src)

def _segment_sum(src, seg, n):
    return jax.ops.segment_sum(src, seg, n)
kernel_name = 'mk_prb_d1_jaxref_r4_4d471f'

def setup_inputs(seed: int=0):
    np.random.seed(seed)
    _w = jnp.asarray

    def _L0_attn_setup():
        import jax, jax.numpy as jnp
        import numpy as np
        B, T, D, N, R = (2, 512, 256, 16, 64)
        key = jax.random.key(seed)
        ks = jax.random.split(key, 8)
        sc = 0.02
        return {'x': jax.random.normal(ks[0], (B, T, D), jnp.float32), 'W_in': jax.random.normal(ks[1], (2 * D, D), jnp.float32) * sc, 'conv_w': jax.random.normal(ks[2], (D, 3), jnp.float32) * sc, 'W_x': jax.random.normal(ks[3], (R + 2 * N, D), jnp.float32) * sc, 'W_dt': jax.random.normal(ks[4], (D, R), jnp.float32) * sc, 'b_dt': jnp.ones((D,), jnp.float32), 'A_log': jnp.full((D, N), -2.0, jnp.float32), 'D_param': jnp.ones((D,), jnp.float32), 'W_C': jax.random.normal(ks[5], (D, N), jnp.float32) * sc, 'W_out': jax.random.normal(ks[6], (D, D), jnp.float32) * sc}
    _L0_attn_in = _L0_attn_setup()

    def _L0_ffn_setup():
        import jax, jax.numpy as jnp
        import numpy as np
        B, C, D = (2, 512, 256)
        I = 512
        E, K = (8, 2)
        CF = 1.25
        key = jax.random.key(seed)
        k1, k2, k3, k4 = jax.random.split(key, 4)
        scale = 0.02
        return {'hidden_states': jax.random.normal(k1, (B, C, D), jnp.float32), 'Wg': jax.random.normal(k2, (E, D), jnp.float32) * scale, 'W1': jax.random.normal(k3, (E, D, 2 * I), jnp.float32) * scale, 'W2': jax.random.normal(k4, (E, I, D), jnp.float32) * scale}
    _L0_ffn_in = _L0_ffn_setup()
    _d = {'L0_attn_x': _L0_attn_in['x'], 'L0_attn_W_in': _L0_attn_in['W_in'], 'L0_attn_conv_w': _L0_attn_in['conv_w'], 'L0_attn_W_x': _L0_attn_in['W_x'], 'L0_attn_W_dt': _L0_attn_in['W_dt'], 'L0_attn_b_dt': _L0_attn_in['b_dt'], 'L0_attn_A_log': _L0_attn_in['A_log'], 'L0_attn_D_param': _L0_attn_in['D_param'], 'L0_attn_W_C': _L0_attn_in['W_C'], 'L0_attn_W_out': _L0_attn_in['W_out'], 'L0_ffn_Wg': _L0_ffn_in['Wg'], 'L0_ffn_W1': _L0_ffn_in['W1'], 'L0_ffn_W2': _L0_ffn_in['W2']}
    _x0 = _d['L0_attn_x']
    _d['L0_attn_x'] = jax.random.normal(jax.random.fold_in(jax.random.key(seed), 1), (1, 4096, 256), dtype=_x0.dtype)
    del _x0
    return _d

def reference(L0_attn_x, L0_attn_W_in, L0_attn_conv_w, L0_attn_W_x, L0_attn_W_dt, L0_attn_b_dt, L0_attn_A_log, L0_attn_D_param, L0_attn_W_C, L0_attn_W_out, L0_ffn_Wg, L0_ffn_W1, L0_ffn_W2):

    def _L0_attn_ref(x, W_in, conv_w, W_x, W_dt, b_dt, A_log, D_param, W_C, W_out):
        import jax, jax.numpy as jnp
        import numpy as np
        B, T, D, N, R = (2, 512, 256, 16, 64)
        xz = jnp.einsum('btd,ed->bte', x, W_in)
        xc, z = jnp.split(xz, 2, axis=-1)
        xp = jnp.pad(xc, ((0, 0), (1, 1), (0, 0)))
        xconv = xp[:, :-2] * conv_w[:, 0] + xp[:, 1:-1] * conv_w[:, 1] + xp[:, 2:] * conv_w[:, 2]
        xs = jax.nn.silu(xconv)
        x_dbl = jnp.einsum('btd,ed->bte', xs, W_x)
        dt_param = x_dbl[..., :R]
        Bp = x_dbl[..., R:R + N]
        Cp = x_dbl[..., R + N:]
        dt = jax.nn.softplus(dt_param @ W_dt.T + b_dt) + 1e-05
        A_disc = jnp.exp(-jnp.exp(A_log)[None, None] * dt[..., None])
        Bx = Bp[:, :, None, :] * dt[..., None] * xs[..., None]
        C = Cp @ W_C.T

        def step(s, inp):
            A_t, Bx_t = inp
            s = A_t * s + Bx_t
            return (s, s.sum(-1))
        s0 = jnp.zeros((x.shape[0], D, N), x.dtype)
        _, ssum = jax.lax.scan(step, s0, (A_disc.transpose(1, 0, 2, 3), Bx.transpose(1, 0, 2, 3)))
        ssum = ssum.transpose(1, 0, 2)
        y = C * ssum + D_param * xs
        return jnp.einsum('btd,ed->bte', y, W_out) * jax.nn.silu(z)

    def _L0_ffn_ref(hidden_states, Wg, W1, W2):
        import jax, jax.numpy as jnp
        import numpy as np
        B, C, D = (2, 512, 256)
        I = 512
        E, K = (8, 2)
        CF = 1.25
        Bx, Cx, d = hidden_states.shape
        N = Bx * Cx
        cap = int(N * K * CF / E)
        x = hidden_states.reshape(N, d)
        logits = x @ Wg.T
        top_v, top_i = jax.lax.top_k(logits, K)
        gates = jax.nn.softmax(top_v, axis=-1)
        flat_e = top_i.reshape(N * K)
        gates_f = gates.reshape(N * K)
        tok = jnp.repeat(jnp.arange(N), K)
        onehot = jax.nn.one_hot(flat_e, E, dtype=jnp.int32)
        pos = jnp.cumsum(onehot, axis=0) - 1
        pos_f = jnp.take_along_axis(pos, flat_e[:, None], axis=1)[:, 0]
        keep = pos_f < cap
        pos_safe = jnp.where(keep, pos_f, cap)
        exp_batches = jnp.zeros((E, cap, d), x.dtype).at[flat_e, pos_safe].set(x[tok], mode='drop')
        h = jnp.einsum('ecd,edf->ecf', exp_batches, W1)
        inp, gate = jnp.split(h, 2, axis=-1)
        h = jax.nn.gelu(inp, approximate=False) * gate
        exp_out = jnp.einsum('eci,eid->ecd', h, W2)
        gathered = exp_out[flat_e, jnp.minimum(pos_safe, cap - 1)]
        contrib = jnp.where(keep, gates_f, 0.0)[:, None] * gathered
        out = jax.ops.segment_sum(contrib, tok, num_segments=N)
        return out.reshape(Bx, Cx, d)
    x = L0_attn_x
    xn = _layernorm(x, axis=-1)
    x = x + _L0_attn_ref(xn, L0_attn_W_in, L0_attn_conv_w, L0_attn_W_x, L0_attn_W_dt, L0_attn_b_dt, L0_attn_A_log, L0_attn_D_param, L0_attn_W_C, L0_attn_W_out) + _L0_ffn_ref(xn, L0_ffn_Wg, L0_ffn_W1, L0_ffn_W2)
    return x

_drawn_inputs = setup_inputs


def setup_inputs(seed=0):
    import zlib

    import numpy as np

    out = dict(_drawn_inputs(seed))
    spreads = {'L0_attn_b_dt': (1.0, 0.6), 'L0_attn_A_log': (-2.0, 0.6), 'L0_attn_D_param': (1.0, 0.6)}
    factors = {'L0_attn_W_in': 8.0,
     'L0_attn_conv_w': 8.0,
     'L0_attn_W_x': 8.0,
     'L0_attn_W_C': 8.0,
     'L0_attn_W_out': 8.0,
     'L0_ffn_Wg': 29.056,
     'L0_ffn_W1': 25.376,
     'L0_ffn_W2': 25.32}
    for name, (base, spread) in spreads.items():
        noise = np.random.default_rng([zlib.crc32(name.encode()), seed]).standard_normal(out[name].shape)
        drawn = base * np.exp(spread * noise) if base else spread * noise
        out[name] = jnp.asarray(drawn.astype(out[name].dtype))
    for name, factor in factors.items():
        out[name] = (out[name] * factor).astype(out[name].dtype)
    return out
```

```python
import concourse.bass as bass
from concourse import mybir
from contextlib import ExitStack

P = 128
T, D, NS, R = 4096, 256, 16, 64
NE, F, CAP = 8, 512, 1280
TC = 512
NCH, TPC, KD = T // TC, TC // P, D // P
QT = 256
NQ, NA = CAP // QT, F // P
NU = KD * NS
EPS = 1e-5
RC = R + NS
CW, CB, CA, CD, CEND = 0, 6, 8, 40, 42
OUT_OF_BOUNDS = 16384


def build(nc, x, w_in, w_out, w_x, w_dtc, wg, par, w1, w2, out):
    f32, f32r, bf16 = mybir.dt.float32, mybir.dt.float32r, mybir.dt.bfloat16
    i32, u32 = mybir.dt.int32, mybir.dt.uint32
    ALU, ACT, AX = mybir.AluOpType, mybir.ActivationFunctionType, mybir.AxisListType.X
    table_in = nc.dram_tensor("expert_in", [NE * CAP, D], f32, kind="Internal").ap()
    table_out = nc.dram_tensor("expert_out", [NE * CAP, D], f32, kind="Internal").ap()
    ctx = ExitStack()
    with ctx:
        def sb(name, shape, dt=f32):
            return ctx.enter_context(nc.sbuf_tensor(name, shape, dt))

        def sem(name):
            return ctx.enter_context(nc.semaphore(name))

        ident = sb("ident", [P, P])
        identb = sb("identb", [P, P], bf16)
        before = sb("before", [P, P], bf16)
        onesb = sb("onesb", [P, P], bf16)
        select = sb("select", [3 * NS, NS, P], bf16)
        desc = sb("desc", [P, TPC, NE])
        w_in_sb = sb("w_in_sb", [P, KD, 2 * D])
        w_out_sb = sb("w_out_sb", [P, KD, D])
        w_x_sb = sb("w_x_sb", [P, KD, R + 2 * NS])
        w_dtc_sb = sb("w_dtc_sb", [RC, D])
        wg_sb = sb("wg_sb", [P, KD, NE])
        par_sb = sb("par_sb", [P, CEND])
        a_neg = sb("a_neg", [P, NU])
        xc = sb("xc", [P, KD, T + 2])
        z = sb("z", [P, T // P, D])
        gate = sb("gate", [P, T // P, 2])
        kept = sb("kept", [P, T // P, 2])
        gap = sb("gap", [P, T // P])
        gidx = sb("gidx", [P, T // P + 2 * TPC, 2], i32)
        region = sb("region", [P, 8192])
        xin = [region[:, h * 1024:(h + 1) * 1024].rearrange("p (j d) -> p j d", d=D) for h in range(2)]
        xn = [region[:, 2048 + h * 1024:3072 + h * 1024].rearrange("p (j d) -> p j d", d=D) for h in range(2)]
        xnT = [region[:, 4096 + h * 1024:5120 + h * 1024].rearrange("p (k t) -> p k t", t=TC) for h in range(2)]
        zeros = region[:, 6144:8192]
        decay = region[:, 0:4096].rearrange("p (u t) -> p u t", t=TC)
        state = region[:, 4096:8192].rearrange("p (g u t) -> p g u t", u=4, t=TC)
        rows = region[:, 0:4096].rearrange("p (h j k d) -> p h j k d", h=2, j=TPC, d=D)
        stats = sb("stats", [P, TPC, 6])
        mv = sb("mv", [P, TPC, 2])
        sd = sb("sd", [P, TPC])
        rstd = sb("rstd", [P, TPC])
        lg = sb("lg", [P, TPC, NE])
        lg2 = sb("lg2", [P, TPC, NE])
        eq = sb("eq", [P, TPC, NE])
        top = sb("top", [P, TPC, 2])
        code = sb("code", [P, TPC, 2])
        hot = sb("hot", [P, TPC, 2, NE])
        hotb = sb("hotb", [P, TPC, NE], bf16)
        base = sb("base", [P, NE])
        pos = sb("pos", [P, TPC, NE])
        hotpos = sb("hotpos", [P, TPC, 2, NE])
        slot = sb("slot", [P, TPC, 2])
        over = sb("over", [P, TPC, 2])
        tmp2 = sb("tmp2", [P, TPC, 2])
        sidx = [sb(f"sidx{h}", [P, TPC * 2], i32) for h in range(2)]
        gst = [sb(f"gst{h}", [P, TPC * 2], i32) for h in range(2)]
        xs = sb("xs", [P, KD, TC])
        proj = sb("proj", [RC, TC])
        dt = sb("dt", [P, KD, TC])
        uu = sb("uu", [P, KD, TC])
        cc = sb("cc", [P, KD, TC])
        dx = sb("dx", [P, KD, TC])
        yy = sb("yy", [P, KD, TC])
        sp = sb("sp", [P, TC])
        rl = sb("rl", [P, TC])
        bsplit = sb("bsplit", [P, TPC, 3 * NS], bf16)
        brest = sb("brest", [P, TPC, NS])
        bT = sb("bT", [3 * NS, TC], bf16)
        drive = sb("drive", [P, 4, TC])
        carry = sb("carry", [P, NU])
        hsum = sb("hsum", [P, TC])
        xres = sb("xres", [P, TPC, D])
        w1_raw = sb("w1_raw", [P, KD, 2 * F])
        w1_hi = sb("w1_hi", [P, KD, 2 * F], f32r)
        w1_lo = sb("w1_lo", [P, KD, 2 * F], f32r)
        w2_sb = sb("w2_sb", [P, NA, D])
        xe = [sb(f"xe{b}", [P, QT // P, D]) for b in range(2)]
        xe_hi = [sb(f"xe_hi{b}", [P, KD, QT], f32r) for b in range(2)]
        xe_lo = [sb(f"xe_lo{b}", [P, KD, QT], f32r) for b in range(2)]
        hh = sb("hh", [P, NA, QT])
        eo = sb("eo", [P, QT // P, D])

        ps = ctx.enter_context(nc.psum_tensor("ps", [P, 8, 512], f32))
        ps_t = ps[:, 0:2, :]
        ps_x = ps[:, 2:4, :]
        ps_z = ps[:, 4:6, :].rearrange("p b (j d) -> p (b j) d", d=D)
        ps_l = ps[:, 6, 0:TPC * NE].rearrange("p (j e) -> p j e", e=NE)
        ps_r = ps[:, 7, 0:TPC * NE].rearrange("p (j e) -> p j e", e=NE)
        ps_c = ps[:, 7, TPC * NE:(TPC + 1) * NE]
        ps_h = ps[:, 0:4, :].rearrange("p a (g t) -> p a g t", t=QT)
        ps_b = ps[:, 4:6, :]
        m0 = ps[:, 6, :]
        m1 = ps[:, 7, :]
        m0b = m0.bitcast(bf16)

        names = """settled v_sum const_ready d_w d_par zero_done x_free0
            var_ready sd_ready xn_ready t_done xnT_ready xc_done xc_kept lg_done hot_ready z_done z_kept
            pos_done idx_ready rows_sent v_self a_self g_self
            pe_t pe_bc pe_s1 pe_s2 pe_dt pe_c pe_xd pe_b pe_bt pe_op
            a_hi a_whi a_dt_read a_abs a_ex a_lg a_c a_proj a_bt a_exp a_gelu a_eo a_xs a_z a_aneg a_gate
            v_lo v_wlo v_dt v_drive v_scan v_conv v_conv_step v_bs v_bs_step v_h v_op v_aneg v_gst v_total v_gate
            g_u g_group g_step g_y g_y_step g_x
            d_raw d_w2 d_xr d_eo""".split()
        S = {n: sem(n) for n in names}
        d_xin = [sem(f"d_xin{h}") for h in range(2)]
        d_scatter = [sem(f"d_scatter{h}") for h in range(2)]
        d_xe = [sem(f"d_xe{b}") for b in range(2)]
        d_gather = [sem(f"d_gather{h}") for h in range(2)]
        d_out = [sem(f"d_out{h}") for h in range(2)]

        def wait(eng, name, value):
            if isinstance(value, int) and value <= 0:
                return
            eng.wait_ge(S[name] if isinstance(name, str) else name, value)

        def settle(eng):
            eng.sem_inc(S["settled"], 1)

        def x_rows(c, n=TPC):
            return x[bass.ds(c * TC, n * P), :].rearrange("(j p) d -> p j d", p=P)

        block = ctx.enter_context(nc.Block())

        @block.sync
        def _(sp_):
            e = sp_

            def load_x(c, h):
                e.dma_start(xin[h], x_rows(c)).then_inc(d_xin[h], 16)

            load_x(0, 0)
            load_x(1, 1)
            e.dma_start(w_in_sb[:, :, :], w_in).then_inc(S["d_w"], 16)
            e.dma_start(wg_sb[:, :, :], wg).then_inc(S["d_w"], 16)
            e.dma_start(par_sb[:, :], par).then_inc(S["d_par"], 16)
            with e.Fori(0, NCH // 2 - 1) as i:
                for h in range(2):
                    e.wait_ge(S["xn_ready"], i * 2 + (h + 1))
                    load_x(i * 2 + (h + 2), h)
            e.dma_start(w_x_sb[:, :, :], w_x).then_inc(S["d_w"], 16)
            e.dma_start(w_out_sb[:, :, :], w_out).then_inc(S["d_w"], 16)
            e.dma_start(w_dtc_sb[:, :], w_dtc).then_inc(S["d_w"], 16)

            def load_w1(i):
                e.dma_start(w1_raw[:, :, :], w1[bass.ds(i * P, P), :].rearrange("p (k f) -> p k f", k=KD)).then_inc(S["d_raw"], 16)

            def load_w2(i):
                e.dma_start(w2_sb[:, :, :], w2[bass.ds(i * P, P), :].rearrange("p (a d) -> p a d", a=NA)).then_inc(S["d_w2"], 16)

            def load_xe(i, q):
                src = table_in[bass.ds(i * CAP + q * QT, QT), :].rearrange("(j p) d -> p j d", p=P)
                e.dma_start(xe[q % 2][:, :, :], src).then_inc(d_xe[q % 2], 16)

            load_w1(0)
            load_w2(0)
            wait(e, "rows_sent", 2 + NCH)
            load_xe(0, 0)

            def step(it, first, last):
                if not last:
                    wait(e, "v_wlo", it * NA + NA)
                    load_w1(it + 1)
                if not first:
                    wait(e, "g_x", it)
                    e.dma_start(xres[:, :, :], x_rows(it - 1)).then_inc(S["d_xr"], 16)
                for q in range(NQ):
                    if q < NQ - 1:
                        wait(e, "pe_t", it * NQ + (q if q else -1))
                        load_xe(it, q + 1)
                    elif not last:
                        wait(e, "pe_t", it * NQ + NQ)
                        load_xe(it + 1, 0)
                    wait(e, "a_eo", it * NQ + (q + 1))
                    dst = table_out[bass.ds(it * CAP + q * QT, QT), :].rearrange("(j p) d -> p j d", p=P)
                    e.dma_start(dst, eo[:, :, :]).then_inc(S["d_eo"], 16)
                if not last:
                    wait(e, "pe_s2", it * NQ + NQ)
                    load_w2(it + 1)

            step(0, True, False)
            with e.Fori(1, NCH - 1) as it:
                step(it, False, False)
            step(NCH - 1, False, True)
            wait(e, "g_x", NCH)
            e.dma_start(xres[:, :, :], x_rows(NCH - 1)).then_inc(S["d_xr"], 16)
            with e.Fori(0, NCH // 2) as i:
                for h in range(2):
                    e.wait_ge(S["v_total"], i * 2 + (h + 3))
                    dst = out[bass.ds((i * 2 + h) * TC, TC), :].rearrange("(j p) d -> p j d", p=P)
                    e.dma_start(dst, z[:, bass.ds((i * 2 + h) * TPC, TPC), :]).then_inc(d_out[h], 16)
            for h in range(2):
                e.wait_ge(d_out[h], 16 * (NCH // 2))
            e.wait_ge(S["d_eo"], 16 * NE * NQ)

        @block.gpsimd
        def _(g):
            cnt = [0]

            def inc(ins):
                cnt[0] += 1
                ins.then_inc(S["const_ready"], 1)

            inc(g.memset(zeros, 0.0))
            inc(g.memset(ident[:, :], 0.0))
            inc(g.memset(before[:, :], 1.0))
            inc(g.memset(onesb[:, :], 1.0))
            inc(g.memset(select[:, :, :], 0.0))
            inc(g.memset(xc[:, :, 0:1], 0.0))
            inc(g.memset(xc[:, :, T + 1:T + 2], 0.0))
            inc(g.memset(carry[:, :], 0.0))
            inc(g.memset(base[:, :], 0.0))
            inc(g.memset(gidx[:, T // P:, :], 0))
            inc(g.iota(desc[:, :, :], pattern=[[0, TPC], [-1, NE]], base=NE, channel_multiplier=0,
                       allow_small_or_imprecise_dtypes=True))
            wait(g, "const_ready", cnt[0])
            inc(g.affine_select(out=ident[:, :], in_=ident[:, :], compare_op=ALU.not_equal, fill=1.0,
                                base=0, pattern=[[-1, P]], channel_multiplier=1))
            inc(g.affine_select(out=before[:, :], in_=before[:, :], compare_op=ALU.is_gt, fill=0.0,
                                base=0, pattern=[[1, P]], channel_multiplier=-1))
            for r in range(3):
                wait(g, "const_ready", cnt[0])
                inc(g.affine_select(out=select[:, :, :], in_=select[:, :, :], compare_op=ALU.not_equal, fill=1.0,
                                    base=-NS * r, pattern=[[-1, NS], [0, P]], channel_multiplier=1))
            wait(g, "const_ready", cnt[0])
            inc(g.tensor_copy(identb[:, :], ident[:, :]))
            assert cnt[0] == N_CONST
            g.sem_inc(S["g_x"], 1)
            g.sem_inc(S["rows_sent"], 2)
            wait(g, "zero_done", 16 * ZERO_DMAS)
            with g.Fori(0, NCH // 2) as i:
                for h in range(2):
                    g.wait_ge(S["idx_ready"], i * 2 + (h + 1))
                    settle(g)
                    for j in range(TPC):
                        for k in range(2):
                            n = 2 * j + k
                            g.indirect_dma_start(table_in, bass.IndirectOffsetOnAxis(ap=sidx[h][:, n:n + 1].bitcast(u32), axis=0),
                                                 xn[h][:, j, :], None, bounds_check=NE * CAP - 1,
                                                 oob_is_err=False).then_inc(d_scatter[h], 16)
                    g.wait_ge(d_scatter[h], i * (32 * TPC) + 32 * TPC)
                    g.sem_inc(S["rows_sent"], 1)

            def drive_job(J, m):
                wait(g, "v_dt", J + 1)
                wait(g, "g_y", J - 1)
                g.tensor_tensor(uu[:, m, :], dt[:, m, :], xs[:, m, :], ALU.mult).then_inc(S["g_u"], 1)
                g.tensor_scalar(dx[:, m, :], xs[:, m, :], par_sb[:, CD + m:CD + m + 1], 0.0, ALU.mult, ALU.add).then_inc(S["g_u"], 1)

            def group(it, G):
                b, m = G % 2, G // 4
                wait(g, "v_scan", it * NU + (4 * G + 4))
                settle(g)
                g.tensor_copy(carry[:, 4 * G:4 * G + 4], state[:, b, :, TC - 1]).then_inc(S["g_step"], 1)
                wait(g, "g_step", it * G_STEPS + group.n + 1)
                g.tensor_tensor(state[:, b, 0:2, :], state[:, b, 0:2, :], state[:, b, 2:4, :], ALU.add).then_inc(S["g_step"], 1)
                wait(g, "g_step", it * G_STEPS + group.n + 2)
                if G % 4 == 0:
                    wait(g, "g_y", it * 2 + m)
                    g.tensor_tensor(hsum[:, :], state[:, b, 0, :], state[:, b, 1, :], ALU.add).then_inc(S["g_group"], 1)
                    group.n += 2
                else:
                    g.tensor_tensor(state[:, b, 0, :], state[:, b, 0, :], state[:, b, 1, :], ALU.add).then_inc(S["g_step"], 1)
                    wait(g, "g_step", it * G_STEPS + group.n + 3)
                    wait(g, "g_group", it * 8 + G)
                    g.tensor_tensor(hsum[:, :], hsum[:, :], state[:, b, 0, :], ALU.add).then_inc(S["g_group"], 1)
                    group.n += 3

            def y_job(it, m):
                J = it * 2 + m
                wait(g, "g_group", it * 8 + 4 * (m + 1))
                wait(g, "a_c", J + 1)
                wait(g, "pe_op", it * 2)
                g.tensor_tensor(hsum[:, :], hsum[:, :], cc[:, m, :], ALU.mult).then_inc(S["g_y_step"], 1)
                wait(g, "g_y_step", J + 1)
                g.tensor_tensor(yy[:, m, :], hsum[:, :], dx[:, m, :], ALU.add).then_inc(S["g_y"], 1)

            def add_x(c):
                wait(g, "v_op", c * 2 + 2)
                wait(g, "d_xr", (c + 1) * 16)
                zc = z[:, bass.ds(c * TPC, TPC), :]
                g.tensor_tensor(zc, zc, xres[:, :, :], ALU.add).then_inc(S["g_x"], 1)

            drive_job(0, 0)

            def step(it, first, last):
                group.n = 0
                drive_job(it * 2 + 1, 1)
                for G in range(8):
                    group(it, G)
                    if G == 3:
                        y_job(it, 0)
                    if G == 4 and not first:
                        add_x(it - 1)
                    if G == 5 and not last:
                        drive_job(it * 2 + 2, 0)
                y_job(it, 1)
                assert group.n == G_STEPS

            step(0, True, False)
            with g.Fori(1, NCH - 1) as it:
                step(it, False, False)
            step(NCH - 1, False, True)
            add_x(NCH - 1)
            g.wait_ge(S["d_eo"], 16 * NE * NQ)
            with g.Fori(0, NCH // 2) as i:
                for h in range(2):
                    g.wait_ge(S["v_gst"], i * 2 + (h + 1))
                    g.wait_ge(S["v_total"], i * 2 + (h + 1))
                    settle(g)
                    for j in range(TPC):
                        for k in range(2):
                            n = 2 * j + k
                            g.indirect_dma_start(rows[:, h, j, k, :], None, table_out,
                                                 bass.IndirectOffsetOnAxis(ap=gst[h][:, n:n + 1].bitcast(u32), axis=0)).then_inc(d_gather[h], 16)

        @block.scalar
        def _(a):
            a.sem_inc(S["xc_kept"], 1)
            wait(a, "const_ready", 1)
            per = 2048
            tin = table_in.rearrange("(p r) d -> p (r d)", p=P)
            for n in range(ZERO_DMAS):
                a.dma_start(tin[:, n * per:(n + 1) * per], zeros).then_inc(S["zero_done"], 16)
            wait(a, "d_par", 16)
            a.activation(a_neg[:, :], par_sb[:, CA:CA + NU], ACT.Exp).then_inc(S["a_aneg"], 1)

            with a.Fori(0, NCH // 2) as i:
                for h in range(2):
                    c = i * 2 + h
                    a.wait_ge(S["var_ready"], c + 1)
                    a.activation(sd[:, :], mv[:, :, 1], ACT.Sqrt).then_inc(S["sd_ready"], 1)
                    a.wait_ge(S["t_done"], c + 1)
                    a.wait_ge(S["z_done"], c + 1)
                    a.activation(xnT[h], ps_t, ACT.Copy).then_inc(S["xnT_ready"], 1)
                    a.wait_ge(S["xc_done"], c + 1)
                    a.activation(xc[:, :, bass.ds(c * TC + 1, TC)], ps_x, ACT.Copy).then_inc(S["xc_kept"], 1)

            def split_w(i, q4, part):
                if q4 is not None:
                    wait(a, "pe_s1", q4 + part + 1)
                if part == 0:
                    wait(a, "d_raw", i * 16 + 16)
                dst = w1_hi[:, :, :].rearrange("p k (g f) -> p k g f", g=2)[:, :, :, part * P:(part + 1) * P]
                src = w1_raw[:, :, :].rearrange("p k (g f) -> p k g f", g=2)[:, :, :, part * P:(part + 1) * P]
                for k in range(KD):
                    a.activation(dst[:, k], src[:, k], ACT.Copy).then_inc(S["a_whi"], 1)

            def dt_job(J, m):
                b = par_sb[:, CB + m:CB + m + 1]
                wait(a, "pe_dt", J + 1)
                wait(a, "v_dt", J)
                a.activation(sp[:, :], m0, ACT.Abs, bias=b).then_inc(S["a_abs"], 1)
                a.activation(rl[:, :], m0, ACT.Relu, bias=b).then_inc(S["a_dt_read"], 1)
                wait(a, "a_abs", J + 1)
                a.activation(sp[:, :], sp[:, :], ACT.Exp, scale=-1.0).then_inc(S["a_ex"], 1)
                wait(a, "a_ex", J + 1)
                a.activation(sp[:, :], sp[:, :], ACT.Ln, bias=1.0).then_inc(S["a_lg"], 1)

            def c_job(J, m):
                wait(a, "pe_c", J + 1)
                wait(a, "g_y", J - 1)
                a.activation(cc[:, m, :], m0, ACT.Copy).then_inc(S["a_c"], 1)

            def silu_xs(c):
                wait(a, "v_conv", c * 2 + 2)
                a.activation(xs[:, :, :], xs[:, :, :], ACT.Silu).then_inc(S["a_xs"], 1)

            def proj_out(c):
                wait(a, "pe_xd", c + 1)
                a.activation(proj[:, :], m0[0:RC, :], ACT.Copy).then_inc(S["a_proj"], 1)

            def bt_out(c):
                wait(a, "pe_bt", c + 1)
                a.activation(bT[:, :], m0b[0:3 * NS, 0:TC], ACT.Copy).then_inc(S["a_bt"], 1)

            a.wait_ge(S["idx_ready"], NCH)
            a.activation(gap[:, :], gap[:, :], ACT.Exp).then_inc(S["a_gate"], 1)
            silu_xs(0)
            for part in range(NA):
                split_w(0, None, part)
            proj_out(0)
            dt_job(0, 0)
            c_job(0, 0)
            bt_out(0)
            wait(a, "rows_sent", 2 + NCH)
            wait(a, "z_done", 2 + NCH)

            def high(it, q):
                wait(a, "pe_t", it * NQ + (q + 1))
                prev = 4 * (q - 1) if q >= 2 else (0 if q == 0 else -4)
                wait(a, "pe_s1", it * (NQ * NA) + prev)
                a.activation(xe_hi[q % 2][:, :, :], m0.rearrange("p (k t) -> p k t", t=QT), ACT.Copy).then_inc(S["a_hi"], 1)

            def exps(it, n):
                for _ in range(n):
                    u = exps.u
                    exps.u += 1
                    if u % NS == 0:
                        wait(a, "v_dt", it * 2 + (u // NS + 1))
                    wait(a, "v_scan", it * NU + (u - 7))
                    a.activation(decay[:, u % 8, :], dt[:, u // NS, :], ACT.Exp, scale=a_neg[:, u:u + 1]).then_inc(S["a_exp"], 1)

            def eo_out(it, q):
                wait(a, "pe_s2", it * NQ + (q + 1))
                wait(a, "d_eo", (it * NQ + q) * 16)
                a.activation(eo[:, :, :], m1.rearrange("p (j d) -> p j d", d=D), ACT.Copy).then_inc(S["a_eo"], 1)

            def step(it, last):
                exps.u = 0
                high(it, 0)
                exps(it, 2)
                dt_job(it * 2 + 1, 1)
                c_job(it * 2 + 1, 1)
                for q in range(NQ):
                    exps(it, 2)
                    if q:
                        eo_out(it, q - 1)
                    exps(it, 2 if q else 1)
                    if q == 1:
                        zc = z[:, bass.ds(it * TPC, TPC), :]
                        if not last:
                            silu_xs(it + 1)
                        a.activation(zc, zc, ACT.Silu).then_inc(S["a_z"], 1)
                    wait(a, "pe_s1", it * (NQ * NA) + NA * (q + 1))
                    wait(a, "pe_s2", it * NQ + q)
                    a.activation(hh[:, :, :], ps_h[:, :, 0, :], ACT.Gelu).then_inc(S["a_gelu"], 1)
                    if q < NQ - 1:
                        high(it, q + 1)
                    if not last:
                        if q == 2:
                            proj_out(it + 1)
                        if q == 3:
                            dt_job(it * 2 + 2, 0)
                            c_job(it * 2 + 2, 0)
                        if q == 4:
                            for part in range(NA):
                                split_w(it + 1, it * (NQ * NA) + 4 * NA, part)
                    exps(it, min(NU - exps.u, 3 if q < 2 else 2))
                assert exps.u == NU
                eo_out(it, NQ - 1)
                if not last:
                    bt_out(it + 1)

            step(0, False)
            with a.Fori(1, NCH - 1) as it:
                step(it, False)
            step(NCH - 1, True)

        @block.vector
        def _(v):
            def norm(c, h, n):
                v.wait_ge(d_xin[h], n * 16 + 16)
                for j in range(TPC):
                    v.bn_stats(stats[:, j, :], xin[h][:, j, :]).then_inc(S["v_self"], 1)
                v.wait_ge(S["v_self"], c * V0 + TPC)
                settle(v)
                for j in range(TPC):
                    v.bn_aggr(mv[:, j, :], stats[:, j, :]).then_inc(S["v_self"], 1)
                v.wait_ge(S["v_self"], c * V0 + 2 * TPC)
                v.tensor_scalar(mv[:, :, 1], mv[:, :, 1], EPS, None, ALU.add).then_inc(S["var_ready"], 1)
                v.wait_ge(S["sd_ready"], c + 1)
                v.reciprocal(rstd[:, :], sd[:, :]).then_inc(S["v_self"], 1)
                v.wait_ge(S["v_self"], c * V0 + 2 * TPC + 1)
                v.wait_ge(S["rows_sent"], c + 1)
                for j in range(TPC):
                    last = v.tensor_scalar(xn[h][:, j, :], xin[h][:, j, :], mv[:, j, 0:1], rstd[:, j:j + 1],
                                           ALU.subtract, ALU.mult)
                last.then_inc(S["xn_ready"], 1)

            def route(c, h):
                n = [0]

                def link(ins):
                    n[0] += 1
                    ins.then_inc(S["g_self"], 1)
                    v.wait_ge(S["g_self"], c * VR + n[0])

                def bc(ap):
                    return ap.unsqueeze(2).to_broadcast([P, TPC, NE])

                v.wait_ge(S["lg_done"], c + 1)
                link(v.tensor_copy(lg[:, :, :], ps_l))
                for k, src in enumerate((lg, lg2)):
                    link(v.tensor_reduce(top[:, :, k], src[:, :, :], AX, ALU.max))
                    link(v.tensor_tensor(eq[:, :, :], src[:, :, :], bc(top[:, :, k]), ALU.is_equal))
                    link(v.tensor_tensor(eq[:, :, :], eq[:, :, :], desc[:, :, :], ALU.mult))
                    link(v.tensor_reduce(code[:, :, k], eq[:, :, :], AX, ALU.max))
                    link(v.tensor_tensor(hot[:, :, k, :], desc[:, :, :], bc(code[:, :, k]), ALU.is_equal))
                    if k == 0:
                        link(v.scalar_tensor_tensor(lg2[:, :, :], hot[:, :, 0, :], -3.0e38, lg[:, :, :], ALU.mult, ALU.add))
                v.tensor_tensor(hotb[:, :, :], hot[:, :, 0, :], hot[:, :, 1, :], ALU.add).then_inc(S["hot_ready"], 1)
                v.tensor_tensor(gap[:, bass.ds(c * TPC, TPC)], top[:, :, 1], top[:, :, 0], ALU.subtract)
                v.wait_ge(S["z_done"], c + 3)
                v.tensor_copy(z[:, bass.ds(c * TPC, TPC), :], ps_z).then_inc(S["z_kept"], 1)
                v.wait_ge(S["pos_done"], c + 1)
                link(v.tensor_tensor(pos[:, :, :], ps_r, base[:, :].unsqueeze(1).to_broadcast([P, TPC, NE]), ALU.add))
                link(v.tensor_tensor(base[:, :], base[:, :], ps_c, ALU.add))
                link(v.tensor_tensor(hotpos[:, :, :, :], hot[:, :, :, :], pos[:, :, :].unsqueeze(2).to_broadcast([P, TPC, 2, NE]), ALU.mult))
                link(v.tensor_reduce(slot[:, :, :], hotpos[:, :, :, :], AX, ALU.add))
                link(v.tensor_scalar(over[:, :, :], slot[:, :, :], float(CAP), float(OUT_OF_BOUNDS), ALU.is_ge, ALU.mult))
                link(v.scalar_tensor_tensor(tmp2[:, :, :], slot[:, :, :], float(NE * CAP), over[:, :, :], ALU.add, ALU.add))
                link(v.scalar_tensor_tensor(sidx[h][:, :].rearrange("p (j k) -> p j k", k=2), code[:, :, :], -float(CAP), tmp2[:, :, :], ALU.mult, ALU.add))
                link(v.tensor_scalar(tmp2[:, :, :], slot[:, :, :], float(CAP - 1), float(NE * CAP), ALU.min, ALU.add))
                link(v.tensor_scalar(kept[:, bass.ds(c * TPC, TPC), :], over[:, :, :], 0.0, None, ALU.is_equal))
                v.scalar_tensor_tensor(gidx[:, bass.ds(c * TPC, TPC), :], code[:, :, :], -float(CAP), tmp2[:, :, :], ALU.mult, ALU.add).then_inc(S["idx_ready"], 1)
                assert n[0] == VR

            v.sem_inc(S["z_kept"], 1)
            v.sem_inc(S["hot_ready"], 1)
            wait(v, "const_ready", N_CONST)
            norm(0, 0, 0)
            with v.Fori(0, NCH // 2 - 1) as i:
                norm(i * 2 + 1, 1, i)
                route(i * 2, 0)
                norm(i * 2 + 2, 0, i + 1)
                route(i * 2 + 1, 1)
            norm(NCH - 1, 1, NCH // 2 - 1)
            route(NCH - 2, 0)
            route(NCH - 1, 1)

            def conv(c):
                wait(v, "g_u", c * 4)
                wait(v, "xc_kept", 1 + NCH)
                n = c * 4
                for tap in range(3):
                    for m in range(KD):
                        src = xc[:, m, bass.ds(c * TC + tap, TC)]
                        w = par_sb[:, CW + 3 * m + tap:CW + 3 * m + tap + 1]
                        if tap == 0:
                            v.tensor_scalar(xs[:, m, :], src, w, None, ALU.mult).then_inc(S["v_conv_step"], 1)
                        else:
                            v.wait_ge(S["v_conv_step"], n + (2 * (tap - 1) + m + 1))
                            v.scalar_tensor_tensor(xs[:, m, :], src, w, xs[:, m, :], ALU.mult, ALU.add)\
                             .then_inc(S["v_conv_step" if tap == 1 else "v_conv"], 1)

            def b_split(c):
                src = m0[:, 0:TPC * NS].rearrange("p (j n) -> p j n", n=NS)
                hi, mid, lo = (bsplit[:, :, r * NS:(r + 1) * NS] for r in range(3))
                wait(v, "pe_b", c + 1)
                v.tensor_copy(hi, src).then_inc(S["v_bs_step"], 1)
                v.wait_ge(S["v_bs_step"], c * 3 + 1)
                v.tensor_tensor(brest[:, :, :], src, hi, ALU.subtract).then_inc(S["v_bs_step"], 1)
                v.wait_ge(S["v_bs_step"], c * 3 + 2)
                v.tensor_copy(mid, brest[:, :, :]).then_inc(S["v_bs_step"], 1)
                v.wait_ge(S["v_bs_step"], c * 3 + 3)
                v.tensor_tensor(lo, brest[:, :, :], mid, ALU.subtract).then_inc(S["v_bs"], 1)

            def dt_out(J, m):
                wait(v, "a_lg", J + 1)
                v.scalar_tensor_tensor(dt[:, m, :], rl[:, :], 1e-5, sp[:, :], ALU.add, ALU.add).then_inc(S["v_dt"], 1)

            def split_w(i, part):
                wait(v, "a_whi", i * (2 * NA) + 2 * (part + 1))
                for k in range(KD):
                    dst, raw, hi = (t[:, :, :].rearrange("p k (g f) -> p k g f", g=2)[:, k, :, part * P:(part + 1) * P]
                                    for t in (w1_lo, w1_raw, w1_hi))
                    last = v.tensor_tensor(dst, raw, hi, ALU.subtract)
                last.then_inc(S["v_wlo"], 1)

            conv(0)
            wait(v, "a_aneg", 1)
            v.tensor_scalar(a_neg[:, :], a_neg[:, :], -1.0, None, ALU.mult).then_inc(S["v_aneg"], 1)
            wait(v, "a_gate", 1)
            v.tensor_scalar(gate[:, :, 0], gap[:, :], 1.0, None, ALU.add).then_inc(S["v_gate"], 1)
            wait(v, "v_gate", 1)
            v.reciprocal(gate[:, :, 0], gate[:, :, 0]).then_inc(S["v_gate"], 1)
            wait(v, "v_gate", 2)
            v.tensor_tensor(gate[:, :, 1], gate[:, :, 0], gap[:, :], ALU.mult).then_inc(S["v_gate"], 1)
            wait(v, "v_gate", 3)
            v.tensor_tensor(gate[:, :, :], gate[:, :, :], kept[:, :, :], ALU.mult).then_inc(S["v_gate"], 1)
            b_split(0)
            for part in range(NA):
                split_w(0, part)
            dt_out(0, 0)
            wait(v, "rows_sent", 2 + NCH)
            wait(v, "z_done", 2 + NCH)

            def low(it, q):
                wait(v, "a_hi", it * NQ + (q + 1))
                v.tensor_tensor(xe_lo[q % 2][:, :, :], m0.rearrange("p (k t) -> p k t", t=QT), xe_hi[q % 2][:, :, :],
                                ALU.subtract).then_inc(S["v_lo"], 1)

            def drive_unit(it, u):
                if u % NS == 0:
                    wait(v, "g_u", (it * 2 + (u // NS + 1)) * 2)
                wait(v, "pe_bc", it * NU + (u + 1))
                v.tensor_tensor(drive[:, u % 4, :], ps_b[:, u % 2, :], uu[:, u // NS, :], ALU.mult).then_inc(S["v_drive"], 1)

            def units(it, n):
                for _ in range(n):
                    u = units.u
                    units.u += 1
                    if u + 1 < NU:
                        drive_unit(it, u + 1)
                    if u % 4 == 0:
                        wait(v, "g_group", it * 8 + (u // 4 - 1))
                    wait(v, "a_exp", it * NU + (u + 1))
                    wait(v, "v_drive", it * NU + (u + 1))
                    v.tensor_tensor_scan(state[:, (u // 4) % 2, u % 4, :], decay[:, u % 8, :], drive[:, u % 4, :],
                                         carry[:, u:u + 1], ALU.mult, ALU.add).then_inc(S["v_scan"], 1)

            def project_out(c, half):
                wait(v, "pe_op", c * 2 + (half + 1))
                wait(v, "a_z", c + 1)
                zc = z[:, bass.ds(c * TPC + 2 * half, 2), :]
                v.tensor_tensor(zc, zc, m1.rearrange("p (j d) -> p j d", d=D), ALU.mult).then_inc(S["v_op"], 1)

            def step(it, first, last):
                units.u = 0
                low(it, 0)
                drive_unit(it, 0)
                units(it, 1)
                dt_out(it * 2 + 1, 1)
                for q in range(NQ):
                    units(it, 4 if q else 3)
                    wait(v, "a_gelu", it * NQ + (q + 1))
                    v.tensor_tensor(hh[:, :, :], hh[:, :, :], ps_h[:, :, 1, :], ALU.mult).then_inc(S["v_h"], 1)
                    if q < NQ - 1:
                        low(it, q + 1)
                    if q == 0 and not last:
                        conv(it + 1)
                    if q in (1, 2) and not first:
                        project_out(it - 1, q - 1)
                    if q == 2 and not last:
                        b_split(it + 1)
                    if q == 3 and not last:
                        dt_out(it * 2 + 2, 0)
                    if q == 4 and not last:
                        for part in range(NA):
                            split_w(it + 1, part)
                    units(it, min(NU - units.u, 3 if q < 2 else 2))
                units(it, NU - units.u)

            step(0, True, False)
            with v.Fori(1, NCH - 1) as it:
                step(it, False, False)
            step(NCH - 1, False, True)
            for half in range(2):
                project_out(NCH - 1, half)

            def next_indices(c, h):
                dst = gst[h][:, :].rearrange("p (j k) -> p j k", k=2)
                v.tensor_copy(dst, gidx[:, bass.ds(c * TPC, TPC), :]).then_inc(S["v_gst"], 1)

            v.sem_inc(S["v_total"], 2)
            for h in range(2):
                next_indices(h, h)
            v.wait_ge(S["g_x"], NCH + 1)
            with v.Fori(0, NCH // 2) as i:
                for h in range(2):
                    c = i * 2 + h
                    v.wait_ge(d_gather[h], i * (32 * TPC) + 32 * TPC)
                    next_indices(c + 2, h)
                    for k in range(2):
                        for j in range(TPC):
                            g = gate[:, bass.ds(c * TPC + j, 1), k]
                            zj = z[:, bass.ds(c * TPC + j, 1), :].rearrange("p j d -> p (j d)")
                            if k == 0:
                                v.scalar_tensor_tensor(rows[:, h, j, 0, :], rows[:, h, j, 0, :], g, zj, ALU.mult, ALU.add).then_inc(S["v_sum"], 1)
                            else:
                                v.wait_ge(S["v_sum"], c * TPC + (j + 1))
                                last = v.scalar_tensor_tensor(zj, rows[:, h, j, 1, :], g, rows[:, h, j, 0, :], ALU.mult, ALU.add)
                    last.then_inc(S["v_total"], 1)

        @block.tensor
        def _(pe):
            mm = nc.tensor.matmul
            pe.sem_inc(S["z_done"], 2)
            wait(pe, "const_ready", N_CONST)
            wait(pe, "d_w", 32)
            with pe.Fori(0, NCH // 2) as i:
                for h in range(2):
                    c = i * 2 + h
                    pe.wait_ge(S["xn_ready"], c + 1)
                    for k in range(KD):
                        for j in range(TPC):
                            last = nc.tensor.transpose(ps_t[:, k, j * P:(j + 1) * P], xn[h][:, j, k * P:(k + 1) * P], ident[:, :])
                    last.then_inc(S["t_done"], 1)
                    pe.wait_ge(S["xnT_ready"], c + 1)
                    pe.wait_ge(S["xc_kept"], c + 1)
                    for m in range(KD):
                        for k in range(KD):
                            last = mm(ps_x[:, m, :], w_in_sb[:, k, m * P:(m + 1) * P], xnT[h][:, k, :], start=k == 0, stop=k == KD - 1)
                    last.then_inc(S["xc_done"], 1)
                    pe.wait_ge(S["hot_ready"], c + 1)
                    for j in range(TPC):
                        for k in range(KD):
                            last = mm(ps_l[:, j, :], xnT[h][:, k, j * P:(j + 1) * P], wg_sb[:, k, :], start=k == 0, stop=k == KD - 1)
                    last.then_inc(S["lg_done"], 1)
                    pe.wait_ge(S["z_kept"], c + 1)
                    for j in range(TPC):
                        for k in range(KD):
                            last = mm(ps_z[:, j, :], xnT[h][:, k, j * P:(j + 1) * P], w_in_sb[:, k, D:2 * D], start=k == 0, stop=k == KD - 1)
                    last.then_inc(S["z_done"], 1)
                    pe.wait_ge(S["hot_ready"], c + 2)
                    for j in range(TPC):
                        mm(ps_r[:, j, :], before[:, :], hotb[:, j, :], start=True, stop=j == 0)
                        for b in range(j):
                            mm(ps_r[:, j, :], onesb[:, :], hotb[:, b, :], start=False, stop=b == j - 1)
                    for j in range(TPC):
                        last = mm(ps_c, onesb[:, :], hotb[:, j, :], start=j == 0, stop=j == TPC - 1)
                    last.then_inc(S["pos_done"], 1)

            def dtc(J, m, prev):
                wait(pe, *prev)
                mm(m0, w_dtc_sb[0:R, m * P:(m + 1) * P], proj[0:R, :], start=True, stop=True).then_inc(S["pe_dt"], 1)
                wait(pe, "a_dt_read", J + 1)
                mm(m0, w_dtc_sb[R:RC, m * P:(m + 1) * P], proj[R:RC, :], start=True, stop=True).then_inc(S["pe_c"], 1)

            def x_dbl(c, prev):
                wait(pe, *prev)
                wait(pe, "a_xs", c + 1)
                for k in range(KD):
                    last = mm(m0[0:RC, :], w_x_sb[:, k, 0:RC], xs[:, k, :], start=k == 0, stop=k == KD - 1)
                last.then_inc(S["pe_xd"], 1)
                wait(pe, "a_proj", c + 1)
                for j in range(TPC):
                    for k in range(KD):
                        last = mm(m0[:, j * NS:(j + 1) * NS], xs[:, k, j * P:(j + 1) * P], w_x_sb[:, k, RC:RC + NS], start=k == 0, stop=k == KD - 1)
                last.then_inc(S["pe_b"], 1)

            def b_transpose(c, prev):
                wait(pe, *prev)
                wait(pe, "v_bs", c + 1)
                settle(pe)
                for j in range(TPC):
                    last = nc.tensor.transpose(m0b[0:3 * NS, j * P:(j + 1) * P], bsplit[:, j, :], identb[:, :])
                last.then_inc(S["pe_bt"], 1)

            wait(pe, "d_w", 80)
            x_dbl(0, ("hot_ready", 1 + NCH))
            dtc(0, 0, ("v_bs", 1))
            b_transpose(0, ("a_c", 1))
            wait(pe, "xc_kept", 1 + NCH)
            wait(pe, "z_kept", 1 + NCH)
            wait(pe, "idx_ready", NCH)

            def transposes(it, q, prev):
                wait(pe, *prev)
                per = 3 if q % 2 == 0 else 2
                wait(pe, d_xe[q % 2], (it * per + (q // 2 + 1)) * 16)
                for k in range(KD):
                    for j in range(QT // P):
                        last = nc.tensor.transpose(m0[:, k * QT + j * P:k * QT + (j + 1) * P], xe[q % 2][:, j, k * P:(k + 1) * P], ident[:, :])
                last.then_inc(S["pe_t"], 1)

            def broadcast(it, n=1):
                for _ in range(n):
                    u = broadcast.u
                    if u == NU:
                        return
                    broadcast.u += 1
                    if u == 0:
                        wait(pe, "a_bt", it + 1)
                    wait(pe, "v_drive", it * NU + (u - 1))
                    mm(ps_b[:, u % 2, :], select[:, u % NS, :], bT[:, :], start=True, stop=True).then_inc(S["pe_bc"], 1)

            def first_product(it, q, a):
                b = q % 2
                if a == 0:
                    wait(pe, "v_h", it * NQ + q)
                    wait(pe, "v_lo", it * NQ + (q + 1))
                if q == 0:
                    wait(pe, "v_wlo", it * NA + (a + 1))
                for part in range(2):
                    c0 = part * F + a * P
                    n = 0
                    for k in range(KD):
                        for w, xx in ((w1_hi, xe_hi), (w1_hi, xe_lo), (w1_lo, xe_hi)):
                            last = mm(ps_h[:, a, part, :], w[:, k, c0:c0 + P], xx[b][:, k, :], start=n == 0, stop=n == 3 * KD - 1)
                            n += 1
                last.then_inc(S["pe_s1"], 1)

            def second_product(it, q, j):
                if j == 0:
                    wait(pe, "v_h", it * NQ + (q + 1))
                    if q == 0:
                        wait(pe, "d_w2", it * 16 + 16)
                for a in range(NA):
                    last = mm(m1[:, j * D:(j + 1) * D], hh[:, a, j * P:(j + 1) * P], w2_sb[:, a, :], start=a == 0, stop=a == NA - 1)
                if j == QT // P - 1:
                    last.then_inc(S["pe_s2"], 1)

            def out_product(c, half):
                wait(pe, "g_y", c * 2 + 2)
                for j in range(2):
                    t0 = (2 * half + j) * P
                    for m in range(KD):
                        last = mm(m1[:, j * D:(j + 1) * D], yy[:, m, t0:t0 + P], w_out_sb[:, m, :], start=m == 0, stop=m == KD - 1)
                last.then_inc(S["pe_op"], 1)

            def step(it, first, last):
                broadcast.u = 0
                broadcast(it, 2)
                transposes(it, 0, ("a_bt", it + 1))
                dtc(it * 2 + 1, 1, ("v_lo", it * NQ + 1))
                for q in range(NQ):
                    for a in range(NA):
                        first_product(it, q, a)
                        broadcast(it)
                    if q == 0:
                        transposes(it, 1, ("a_c", it * 2 + 2))
                    elif q == NQ - 1:
                        pass
                    elif q == 3 and not last:
                        transposes(it, q + 1, ("v_bs", it + 2))
                    else:
                        transposes(it, q + 1, ("v_lo", it * NQ + (q + 1)))
                    broadcast(it)
                    if q in (1, 2) and not first:
                        wait(pe, "a_eo", it * NQ + q)
                        out_product(it - 1, q - 1)
                    if q == 2 and not last:
                        x_dbl(it + 1, ("v_lo", it * NQ + 4))
                    if q == 3 and not last:
                        dtc(it * 2 + 2, 0, ("v_lo", it * NQ + 5))
                    if q in (1, 2) and not first:
                        wait(pe, "v_op", (it - 1) * 2 + q)
                    else:
                        wait(pe, "a_eo", it * NQ + q)
                    for j in range(QT // P):
                        second_product(it, q, j)
                        if not (q >= 2 and j == 1):
                            broadcast(it)
                assert broadcast.u == NU
                if not last:
                    b_transpose(it + 1, ("a_c", it * 2 + 3))

            step(0, True, False)
            with pe.Fori(1, NCH - 1) as it:
                step(it, False, False)
            step(NCH - 1, False, True)
            wait(pe, "a_eo", NCH * NQ)
            out_product(NCH - 1, 0)
            wait(pe, "v_op", 2 * NCH - 1)
            out_product(NCH - 1, 1)


N_CONST = 17
ZERO_DMAS = NE * CAP * D // P // 2048
V0 = 2 * TPC + 1
VR = 21
G_STEPS = 22


def kernel(**inputs):
    import numpy as np
    import concourse.bacc as bacc
    from concourse.bass_utils import run_bass_kernel_spmd

    def cols(w):
        w = np.asarray(w)
        return np.ascontiguousarray(w.reshape(KD, P, -1).transpose(1, 0, 2))

    i = {k: np.asarray(v) for k, v in inputs.items()}
    w_x = i["L0_attn_W_x"]
    w_x = np.concatenate([w_x[:R], w_x[R + NS:], w_x[R:R + NS]], axis=0)
    par = np.concatenate([cols(i["L0_attn_conv_w"]).reshape(P, -1), cols(i["L0_attn_b_dt"]).reshape(P, -1),
                          cols(i["L0_attn_A_log"]).reshape(P, -1), cols(i["L0_attn_D_param"]).reshape(P, -1)], axis=1)
    arrays = {
        "x": np.ascontiguousarray(i["L0_attn_x"].reshape(T, D)),
        "w_in": cols(i["L0_attn_W_in"].T),
        "w_out": cols(i["L0_attn_W_out"].T),
        "w_x": cols(w_x.T),
        "w_dtc": np.ascontiguousarray(np.concatenate([i["L0_attn_W_dt"].T, i["L0_attn_W_C"].T], axis=0)),
        "wg": cols(i["L0_ffn_Wg"].T),
        "par": np.ascontiguousarray(par),
        "w1": np.ascontiguousarray(i["L0_ffn_W1"].reshape(NE, KD, P, 2 * F).transpose(0, 2, 1, 3).reshape(NE * P, -1)),
        "w2": np.ascontiguousarray(i["L0_ffn_W2"].reshape(NE, NA, P, D).transpose(0, 2, 1, 3).reshape(NE * P, -1)),
    }
    nc = bacc.Bacc("TRN2", target_bir_lowering=False, num_devices=1)
    f32 = mybir.dt.float32
    aps = [nc.dram_tensor(n, a.shape, f32, kind="ExternalInput").ap() for n, a in arrays.items()]
    out = nc.dram_tensor("out", [T, D], f32, kind="ExternalOutput").ap()
    build(nc, *aps, out)
    r = run_bass_kernel_spmd(nc, [arrays], core_ids=[0])
    return r.results[0]["out"].reshape(1, T, D)
```

```python
import concourse.bass as bass
from concourse import mybir
from contextlib import ExitStack

P = 128
T, D, NS, R = 4096, 256, 16, 64
NE, F, CAP = 8, 512, 1280
TC = 512
NCH, TPC, KD = T // TC, TC // P, D // P
QT = 256
NQ, NA = CAP // QT, F // P
NU = KD * NS
EPS = 1e-5
RC = R + NS
CW, CB, CA, CD, CEND = 0, 6, 8, 40, 42
OUT_OF_BOUNDS = 16384
DX = D + 2


def build(nc, x, w_in, w_out, w_x, w_dtc, wg, par, w1, w2, out):
    f32, f32r, bf16 = mybir.dt.float32, mybir.dt.float32r, mybir.dt.bfloat16
    i32, u32 = mybir.dt.int32, mybir.dt.uint32
    ALU, ACT, AX = mybir.AluOpType, mybir.ActivationFunctionType, mybir.AxisListType.X
    table_in = nc.dram_tensor("expert_in", [NE * CAP, DX], f32, kind="Internal").ap()
    table_out = nc.dram_tensor("expert_out", [2 * T, D], f32, kind="Internal").ap()
    ctx = ExitStack()
    with ctx:
        def sb(name, shape, dt=f32):
            return ctx.enter_context(nc.sbuf_tensor(name, shape, dt))

        def sem(name):
            return ctx.enter_context(nc.semaphore(name))

        ident = sb("ident", [P, P])
        identb = sb("identb", [P, P], bf16)
        select = sb("select", [3 * NS, NS, P], bf16)
        desc = sb("desc", [P, TPC, NE])
        w_in_sb = sb("w_in_sb", [P, KD, 2 * D])
        w_out_sb = sb("w_out_sb", [P, KD, D])
        w_x_sb = sb("w_x_sb", [P, KD, R + 2 * NS])
        w_dtc_sb = sb("w_dtc_sb", [RC, D])
        wg_sb = sb("wg_sb", [P, KD, NE])
        par_sb = sb("par_sb", [P, CEND])
        a_neg = sb("a_neg", [P, NU])
        xc = sb("xc", [P, KD, T + 2])
        z = sb("z", [P, T // P, D])
        gate = sb("gate", [P, T // P, 2])
        kept = sb("kept", [P, T // P, 2])
        gap = sb("gap", [P, T // P])
        tag = sb("tag", [P, T // P])
        region = sb("region", [P, 8192])
        xin = [region[:, h * 1024:(h + 1) * 1024].rearrange("p (j d) -> p j d", d=D) for h in range(3)]
        xn = [region[:, 3072 + h * TPC * DX:3072 + (h + 1) * TPC * DX].rearrange("p (j d) -> p j d", d=DX) for h in range(3)]
        xnT = region[:, 6168:7192].rearrange("p (k t) -> p k t", t=TC)
        zeros = z[:, T // P - 7:, :].rearrange("p j d -> p (j d)")[:, 0:NZ]
        decay = region[:, 0:4096].rearrange("p (u t) -> p u t", t=TC)
        state = region[:, 4096:8192].rearrange("p (g u t) -> p g u t", u=4, t=TC)
        cc = sb("cc", [P, KD, TC])
        cc_flat = cc[:, :, :].rearrange("p m t -> p (m t)")
        used = [0]

        def small(shape, dt=f32):
            n = 1
            for d in shape[1:]:
                n *= d
            words = n // 2 if dt == bf16 else n
            ap = cc_flat[:, used[0]:used[0] + words]
            used[0] += words
            assert used[0] <= KD * TC
            if dt == bf16:
                ap = ap.bitcast(bf16)
            if len(shape) == 3:
                return ap.rearrange("p (a b) -> p a b", b=shape[2])
            if len(shape) == 4:
                return ap.rearrange("p (a b c) -> p a b c", b=shape[2], c=shape[3])
            return ap

        before = small([P, P], bf16)
        onesb = small([P, P], bf16)
        stats = small([P, TPC, 6])
        mv = small([P, TPC, 2])
        sd = small([P, TPC])
        rstd = small([P, TPC])
        lg = small([P, TPC, NE])
        lg2 = small([P, TPC, NE])
        eq = small([P, TPC, NE])
        top = small([P, TPC, 2])
        code = small([P, TPC, 2])
        hot = small([P, TPC, 2, NE])
        hotb = small([P, TPC, NE], bf16)
        base = sb("base", [P, NE])
        pos = small([P, TPC, NE])
        hotpos = small([P, TPC, 2, NE])
        slot = small([P, TPC, 2])
        over = small([P, TPC, 2])
        tmp2 = small([P, TPC, 2])
        sidx = [sb(f"sidx{h}", [P, TPC * 2], i32) for h in range(3)]
        xs = sb("xs", [P, KD, TC])
        proj = sb("proj", [RC, TC])
        dt = sb("dt", [P, KD, TC])
        uu = sb("uu", [P, KD, TC])
        dx = sb("dx", [P, KD, TC])
        yy = sb("yy", [P, KD, TC])
        sp = sb("sp", [P, TC])
        bsplit = sb("bsplit", [P, TPC, 3 * NS], bf16)
        brest = sb("brest", [P, TPC, NS])
        bT = sb("bT", [3 * NS, TC], bf16)
        drive = sb("drive", [P, 3, TC])
        carry = sb("carry", [P, NU])
        hsum = sb("hsum", [P, TC])
        xres = w_in_sb[:, :, :].rearrange("p k (j d) -> p (k j) d", d=D)
        w1_raw = sb("w1_raw", [P, KD, 2 * F])
        w1_hi = sb("w1_hi", [P, KD, 2 * F], f32r)
        w1_lo = sb("w1_lo", [P, KD, 2 * F], f32r)
        w2_sb = sb("w2_sb", [P, NA, D])
        xe = [sb(f"xe{b}", [P, QT // P, DX]) for b in range(3)]
        xe_hi = [sb(f"xe_hi{b}", [P, KD, QT], f32r) for b in range(2)]
        xe_lo = [sb(f"xe_lo{b}", [P, KD, QT], f32r) for b in range(2)]
        hh = [sb(f"hh{b}", [P, NA, QT]) for b in range(3)]
        eo = [sb(f"eo{b}", [P, QT // P, D]) for b in range(3)]
        rows = [[t.rearrange("p (j d) -> p j d", d=D) for t in pair] for pair in
                ([w1_raw[:, k, :] for k in range(2)], [hh[b][:, :, :].rearrange("p a t -> p (a t)") for b in range(2)],
                 [region[:, k * 1024:(k + 1) * 1024] for k in range(2)], [region[:, k * 1024:(k + 1) * 1024] for k in range(2, 4)])]
        second = sb("second", [P, QT // P])
        oidx_sb = sb("oidx", [P, NQ, QT // P], i32)
        oidx = [oidx_sb[:, q, :] for q in range(NQ)]

        ps = ctx.enter_context(nc.psum_tensor("ps", [P, 8, 512], f32))
        ps_t = ps[:, 0:2, :]
        ps_x = ps[:, 2:4, :]
        ps_z = ps[:, 4:6, :].rearrange("p b (j d) -> p (b j) d", d=D)
        ps_l = ps[:, 6, 0:TPC * NE].rearrange("p (j e) -> p j e", e=NE)
        ps_r = ps[:, 7, 0:TPC * NE].rearrange("p (j e) -> p j e", e=NE)
        ps_c = ps[:, 7, TPC * NE:(TPC + 1) * NE]
        ps_h = ps[:, 0:4, :].rearrange("p a (g t) -> p a g t", t=QT)
        ps_b = ps[:, 4:6, :]
        m0 = ps[:, 6, :]
        m1 = ps[:, 7, :]
        m0b = m0.bitcast(bf16)

        names = """settled v_sum v_tag const_ready d_w d_par zero_done zero_out
            var_ready sd_ready xn_ready t_done xnT_ready xc_done xc_kept lg_done hot_ready z_done z_kept
            pos_done idx_ready rows_sent v_self a_self g_self
            pe_t pe_bc pe_s1 pe_s2 pe_dt pe_c pe_xd pe_b pe_bt pe_op
            a_hi a_whi a_dt_read a_abs a_ex a_lg a_c a_proj a_bt a_exp a_gelu a_eo a_xs a_z a_aneg a_gate
            v_lo v_wlo v_dt v_drive v_scan v_conv v_conv_step v_bs v_bs_step v_h v_op v_aneg v_oidx v_total v_gate
            g_u g_group g_step g_y g_y_step g_x
            d_raw d_w2 d_xr""".split()
        S = {n: sem(n) for n in names}
        d_xin = [sem(f"d_xin{h}") for h in range(3)]
        d_scatter = [sem(f"d_scatter{h}") for h in range(3)]
        d_xe = [sem(f"d_xe{b}") for b in range(3)]
        d_send = [sem(f"d_send{b}") for b in range(3)]
        d_rows = [sem(f"d_rows{b}") for b in range(4)]
        d_out = [sem(f"d_out{h}") for h in range(2)]

        def wait(eng, name, value):
            if isinstance(value, int) and value <= 0:
                return
            eng.wait_ge(S[name] if isinstance(name, str) else name, value)

        def buffer(it, q):
            return BUF[q], it * BUF.count(BUF[q]) + BUF[:q].count(BUF[q])

        def wait_scatters(eng):
            for h in range(3):
                eng.wait_ge(d_scatter[h], 32 * TPC * len(range(h, NCH, 3)))

        def settle(eng):
            eng.sem_inc(S["settled"], 1)

        def x_rows(c, n=TPC):
            return x[bass.ds(c * TC, n * P), :].rearrange("(j p) d -> p j d", p=P)

        block = ctx.enter_context(nc.Block())

        @block.sync
        def _(sp_):
            e = sp_

            def load_x(c, h):
                e.dma_start(xin[h], x_rows(c)).then_inc(d_xin[h], 16)

            load_x(0, 0)
            e.dma_start(par_sb[:, :], par).then_inc(S["d_par"], 16)
            e.dma_start(w_in_sb[:, :, :], w_in).then_inc(S["d_w"], 16)
            e.dma_start(wg_sb[:, :, :], wg).then_inc(S["d_w"], 16)
            load_x(1, 1)
            load_x(2, 2)
            for c in range(3, NCH):
                e.wait_ge(S["xn_ready"], c - 2)
                load_x(c, c % 3)
            e.dma_start(w_x_sb[:, :, :], w_x).then_inc(S["d_w"], 16)
            e.dma_start(w_out_sb[:, :, :], w_out).then_inc(S["d_w"], 16)
            e.dma_start(w_dtc_sb[:, :], w_dtc).then_inc(S["d_w"], 16)

            def load_w1(i):
                e.dma_start(w1_raw[:, :, :], w1[bass.ds(i * P, P), :].rearrange("p (k f) -> p k f", k=KD)).then_inc(S["d_raw"], 16)

            def load_w2(i):
                e.dma_start(w2_sb[:, :, :], w2[bass.ds(i * P, P), :].rearrange("p (a d) -> p a d", a=NA)).then_inc(S["d_w2"], 16)

            def load_xe(i, q):
                src = table_in[bass.ds(i * CAP + q * QT, QT), :].rearrange("(j p) d -> p j d", p=P)
                e.dma_start(xe[BUF[q]][:, :, :], src).then_inc(d_xe[BUF[q]], 16)

            load_w1(0)
            load_w2(0)
            wait_scatters(e)
            load_xe(0, 0)
            load_xe(0, 1)

            def next_xe(it, q):
                wait(e, "pe_t", it * NQ + (q - 1))
                wait(e, "v_oidx", it * NQ + (q - 1))
                load_xe(it + q // NQ, q % NQ)

            def step(it, first, last):
                if not first:
                    wait(e, "pe_s2", it * NQ)
                    load_w2(it)
                    wait(e, "g_x", it)
                    e.dma_start(xres, x_rows(it - 1)).then_inc(S["d_xr"], 16)
                next_xe(it, 2)
                if not last:
                    wait(e, "v_wlo", it * NA + NA)
                    load_w1(it + 1)
                for q in range(3, NQ if last else NQ + 2):
                    next_xe(it, q)

            step(0, True, False)
            with e.Fori(1, NCH - 1) as it:
                step(it, False, False)
            step(NCH - 1, False, True)
            wait(e, "g_x", NCH)
            e.dma_start(xres, x_rows(NCH - 1)).then_inc(S["d_xr"], 16)
            for b in range(3):
                e.wait_ge(d_send[b], 32 * NE * BUF.count(b))
            wait(e, "v_wlo", NCH * NA)
            for c in range(NCH):
                if c == 1:
                    wait(e, "pe_s2", NCH * NQ - 1)
                if c == 2:
                    wait(e, "v_scan", NCH * NU)
                if c >= 4:
                    e.wait_ge(S["v_total"], c - 3)
                for k in range(2):
                    src = table_out[c * TC + k * T:(c + 1) * TC + k * T, :].rearrange("(j p) d -> p j d", p=P)
                    e.dma_start(rows[c % 4][k], src).then_inc(d_rows[c % 4], 16)

        @block.gpsimd
        def _(g):
            cnt = [0]

            def inc(ins):
                cnt[0] += 1
                ins.then_inc(S["const_ready"], 1)

            inc(g.memset(zeros, 0.0))
            inc(g.memset(ident[:, :], 0.0))
            wait(g, "const_ready", cnt[0])
            inc(g.affine_select(out=ident[:, :], in_=ident[:, :], compare_op=ALU.not_equal, fill=1.0,
                                base=0, pattern=[[-1, P]], channel_multiplier=1))
            assert cnt[0] == N_IDENT
            inc(g.memset(before[:, :], 1.0))
            inc(g.memset(onesb[:, :], 1.0))
            inc(g.memset(select[:, :, :], 0.0))
            inc(g.memset(xc[:, :, 0:1], 0.0))
            inc(g.memset(xc[:, :, T + 1:T + 2], 0.0))
            inc(g.memset(carry[:, :], 0.0))
            inc(g.memset(base[:, :], 0.0))
            inc(g.iota(tag[:, :], pattern=[[P, T // P]], base=-OUT_OF_BOUNDS, channel_multiplier=1,
                       allow_small_or_imprecise_dtypes=True))
            inc(g.iota(desc[:, :, :], pattern=[[0, TPC], [-1, NE]], base=NE, channel_multiplier=0,
                       allow_small_or_imprecise_dtypes=True))
            wait(g, "const_ready", cnt[0])
            inc(g.affine_select(out=before[:, :], in_=before[:, :], compare_op=ALU.is_gt, fill=0.0,
                                base=0, pattern=[[1, P]], channel_multiplier=-1))
            for r in range(3):
                wait(g, "const_ready", cnt[0])
                inc(g.affine_select(out=select[:, :, :], in_=select[:, :, :], compare_op=ALU.not_equal, fill=1.0,
                                    base=-NS * r, pattern=[[-1, NS], [0, P]], channel_multiplier=1))
            wait(g, "const_ready", cnt[0])
            inc(g.tensor_copy(identb[:, :], ident[:, :]))
            assert cnt[0] == N_CONST
            g.sem_inc(S["g_x"], 1)
            g.sem_inc(S["rows_sent"], 3)
            wait(g, "zero_done", 16 * ZERO_DMAS)

            def scatter(c, h):
                g.wait_ge(S["idx_ready"], c + 1)
                settle(g)
                for n in range(2 * TPC):
                    g.indirect_dma_start(table_in, bass.IndirectOffsetOnAxis(ap=sidx[h][:, n:n + 1].bitcast(u32), axis=0),
                                         xn[h][:, n // 2, :], None, bounds_check=NE * CAP - 1,
                                         oob_is_err=False).then_inc(d_scatter[h], 16)

            with g.Fori(0, 2) as i:
                for h in range(3):
                    scatter(i * 3 + h, h)
                    for done in ((), (0,), (1, 2))[h]:
                        g.wait_ge(d_scatter[done], (i + 1) * (32 * TPC))
                        g.sem_inc(S["rows_sent"], 1)
            scatter(6, 0)
            scatter(7, 1)

            def drive_job(J, m):
                wait(g, "v_dt", J + 1)
                wait(g, "g_y", J - 1)
                g.tensor_tensor(uu[:, m, :], dt[:, m, :], xs[:, m, :], ALU.mult).then_inc(S["g_u"], 1)
                g.tensor_scalar(dx[:, m, :], xs[:, m, :], par_sb[:, CD + m:CD + m + 1], 0.0, ALU.mult, ALU.add).then_inc(S["g_u"], 1)

            def group(it, G):
                b, m = G % 2, G // 4
                wait(g, "v_scan", it * NU + (4 * G + 4))
                settle(g)
                g.tensor_copy(carry[:, 4 * G:4 * G + 4], state[:, b, :, TC - 1]).then_inc(S["g_step"], 1)
                wait(g, "g_step", it * G_STEPS + group.n + 1)
                g.tensor_tensor(state[:, b, 0:2, :], state[:, b, 0:2, :], state[:, b, 2:4, :], ALU.add).then_inc(S["g_step"], 1)
                wait(g, "g_step", it * G_STEPS + group.n + 2)
                if G % 4 == 0:
                    wait(g, "g_y", it * 2 + m)
                    g.tensor_tensor(hsum[:, :], state[:, b, 0, :], state[:, b, 1, :], ALU.add).then_inc(S["g_group"], 1)
                    group.n += 2
                else:
                    g.tensor_tensor(state[:, b, 0, :], state[:, b, 0, :], state[:, b, 1, :], ALU.add).then_inc(S["g_step"], 1)
                    wait(g, "g_step", it * G_STEPS + group.n + 3)
                    wait(g, "g_group", it * 8 + G)
                    g.tensor_tensor(hsum[:, :], hsum[:, :], state[:, b, 0, :], ALU.add).then_inc(S["g_group"], 1)
                    group.n += 3

            def y_job(it, m):
                J = it * 2 + m
                wait(g, "g_group", it * 8 + 4 * (m + 1))
                wait(g, "a_c", J + 1)
                wait(g, "pe_op", it * 2)
                g.tensor_tensor(hsum[:, :], hsum[:, :], cc[:, m, :], ALU.mult).then_inc(S["g_y_step"], 1)
                wait(g, "g_y_step", J + 1)
                g.tensor_tensor(yy[:, m, :], hsum[:, :], dx[:, m, :], ALU.add).then_inc(S["g_y"], 1)

            def add_x(c):
                wait(g, "v_op", c * 2 + 2)
                wait(g, "d_xr", (c + 1) * 16)
                zc = z[:, bass.ds(c * TPC, TPC), :]
                g.tensor_tensor(zc, zc, xres, ALU.add).then_inc(S["g_x"], 1)

            def send(it, q):
                b, before_ = buffer(it, q)
                wait(g, "a_eo", it * NQ + (q + 1))
                wait(g, "v_oidx", it * NQ + (q + 1))
                settle(g)
                for j in range(QT // P):
                    g.indirect_dma_start(table_out, bass.IndirectOffsetOnAxis(ap=oidx[q][:, j:j + 1].bitcast(u32), axis=0),
                                         eo[b][:, j, :], None, bounds_check=2 * T - 1, oob_is_err=False).then_inc(d_send[b], 16)

            drive_job(0, 0)

            def step(it, first, last):
                group.n = 0
                for G in range(8):
                    if G == 2:
                        drive_job(it * 2 + 1, 1)
                    if G in (0, 1) and not first:
                        send(it - 1, 3 + G)
                    if G == 3:
                        if first:
                            wait(g, "zero_out", 16 * ZERO_OUT_DMAS)
                        send(it, 0)
                    group(it, G)
                    if G == 3:
                        y_job(it, 0)
                    if G == 4 and not first:
                        add_x(it - 1)
                    if G == 4:
                        send(it, 1)
                    if G == 5 and not last:
                        drive_job(it * 2 + 2, 0)
                    if G == 6:
                        send(it, 2)
                if last:
                    send(it, 3)
                    send(it, 4)
                y_job(it, 1)
                assert group.n == G_STEPS

            step(0, True, False)
            with g.Fori(1, NCH - 1) as it:
                step(it, False, False)
            step(NCH - 1, False, True)
            add_x(NCH - 1)

        @block.scalar
        def _(a):
            a.sem_inc(S["xc_kept"], 1)
            a.sem_inc(S["z_kept"], 1)
            wait(a, "const_ready", 1)
            tin = table_in.rearrange("(p r) d -> p (r d)", p=P)
            for n in range(ZERO_DMAS):
                a.dma_start(tin[:, n * NZ:(n + 1) * NZ], zeros).then_inc(S["zero_done"], 16)
            tout = table_out.rearrange("(p r) d -> p (r d)", p=P)
            for n in range(ZERO_OUT_DMAS):
                a.dma_start(tout[:, n * NZO:(n + 1) * NZO], zeros[:, 0:NZO]).then_inc(S["zero_out"], 16)
            wait(a, "d_par", 16)
            a.activation(a_neg[:, :], par_sb[:, CA:CA + NU], ACT.Exp).then_inc(S["a_aneg"], 1)

            def deviation(c):
                a.wait_ge(S["var_ready"], c + 1)
                a.activation(sd[:, :], mv[:, :, 1], ACT.Sqrt).then_inc(S["sd_ready"], 1)

            def keep_xnT(c):
                a.wait_ge(S["t_done"], c + 1)
                a.activation(xnT, ps_t, ACT.Copy).then_inc(S["xnT_ready"], 1)

            def keep_xc(c):
                a.wait_ge(S["xc_done"], c + 1)
                a.activation(xc[:, :, bass.ds(c * TC + 1, TC)], ps_x, ACT.Copy).then_inc(S["xc_kept"], 1)

            def keep_z(c):
                a.wait_ge(S["z_done"], c + 1)
                a.activation(z[:, bass.ds(c * TPC, TPC), :], ps_z, ACT.Copy).then_inc(S["z_kept"], 1)

            def keep(c):
                keep_xc(c)
                keep_z(c)
                if isinstance(c, int) and c == NCH - 1:
                    return
                keep_xnT(c + 1)
                if isinstance(c, int) and c == NCH - 2:
                    return
                deviation(c + 2)

            deviation(0)
            keep_xnT(0)
            deviation(1)
            with a.Fori(0, 2) as i:
                for h in range(3):
                    keep(i * 3 + h)
            wait(a, "zero_done", 16 * ZERO_DMAS)
            wait(a, "zero_out", 16 * ZERO_OUT_DMAS)
            keep(NCH - 2)
            keep(NCH - 1)

            def split_w(i, q4, part):
                if q4 is not None:
                    wait(a, "pe_s1", q4 + part + 1)
                if part == 0:
                    wait(a, "d_raw", i * 16 + 16)
                dst = w1_hi[:, :, :].rearrange("p k (g f) -> p k g f", g=2)[:, :, :, part * P:(part + 1) * P]
                src = w1_raw[:, :, :].rearrange("p k (g f) -> p k g f", g=2)[:, :, :, part * P:(part + 1) * P]
                for k in range(KD):
                    a.activation(dst[:, k], src[:, k], ACT.Copy).then_inc(S["a_whi"], 1)

            def dt_job(J, m):
                b = par_sb[:, CB + m:CB + m + 1]
                wait(a, "pe_dt", J + 1)
                wait(a, "v_dt", J)
                wait(a, "g_u", 2 * J - 2)
                a.activation(sp[:, :], m0, ACT.Abs, bias=b).then_inc(S["a_abs"], 1)
                a.activation(dt[:, m, :], m0, ACT.Relu, bias=b).then_inc(S["a_dt_read"], 1)
                wait(a, "a_abs", J + 1)
                a.activation(sp[:, :], sp[:, :], ACT.Exp, scale=-1.0).then_inc(S["a_ex"], 1)
                wait(a, "a_ex", J + 1)
                a.activation(sp[:, :], sp[:, :], ACT.Ln, bias=1.0).then_inc(S["a_lg"], 1)

            def c_job(J, m):
                wait(a, "pe_c", J + 1)
                wait(a, "g_y", J - 1)
                a.activation(cc[:, m, :], m0, ACT.Copy).then_inc(S["a_c"], 1)

            def silu_xs(c):
                wait(a, "v_conv", c * 2 + 2)
                a.activation(xs[:, :, :], xs[:, :, :], ACT.Silu).then_inc(S["a_xs"], 1)

            def proj_out(c):
                wait(a, "pe_xd", c + 1)
                a.activation(proj[:, :], m0[0:RC, :], ACT.Copy).then_inc(S["a_proj"], 1)

            def bt_out(c):
                wait(a, "pe_bt", c + 1)
                a.activation(bT[:, :], m0b[0:3 * NS, 0:TC], ACT.Copy).then_inc(S["a_bt"], 1)

            silu_xs(0)
            for part in range(NA):
                split_w(0, None, part)
            proj_out(0)
            a.wait_ge(S["hot_ready"], 1 + NCH)
            a.activation(gap[:, :], gap[:, :], ACT.Exp).then_inc(S["a_gate"], 1)
            dt_job(0, 0)
            wait(a, "idx_ready", NCH)
            c_job(0, 0)
            bt_out(0)
            wait_scatters(a)

            def high(it, q):
                wait(a, "pe_t", it * NQ + (q + 1))
                a.activation(xe_hi[q % 2][:, :, :], m0.rearrange("p (k t) -> p k t", t=QT), ACT.Copy).then_inc(S["a_hi"], 1)

            def exps(it, n):
                for _ in range(min(n, NU - exps.u)):
                    u = exps.u
                    exps.u += 1
                    if u % NS == 0:
                        wait(a, "v_dt", it * 2 + (u // NS + 1))
                    wait(a, "v_scan", it * NU + (u - 7))
                    a.activation(decay[:, u % 8, :], dt[:, u // NS, :], ACT.Exp, scale=a_neg[:, u:u + 1]).then_inc(S["a_exp"], 1)

            def eo_out(it, q):
                b, uses = buffer(it, q)
                wait(a, "pe_s2", it * NQ + (q + 1))
                wait(a, d_send[b], uses * 32)
                a.activation(eo[b][:, :, :], m1.rearrange("p (j d) -> p j d", d=D), ACT.Copy).then_inc(S["a_eo"], 1)

            high(0, 0)

            def step(it, first, last):
                exps.u = 0
                exps(it, 4)
                for q in range(NQ):
                    if q >= 2:
                        eo_out(it, q - 2)
                    elif not first:
                        eo_out(it - 1, q + 3)
                    if q == 3 and not last:
                        proj_out(it + 1)
                    exps(it, 2)
                    if q == 1:
                        c_job(it * 2 + 1, 1)
                    if q == 4 and not last:
                        c_job(it * 2 + 2, 0)
                    if q < 3:
                        high(it, q + 1)
                    exps(it, 2 if q else 1)
                    wait(a, "pe_s2", it * NQ + (q - 1))
                    for half in range(2):
                        wait(a, "pe_s1", (it * NQ + q) * NA + (2 * half + 2))
                        a.activation(hh[BUF[q]][:, 2 * half:2 * half + 2, :], ps_h[:, 2 * half:2 * half + 2, 0, :], ACT.Gelu).then_inc(S["a_gelu"], 1)
                    if q == 0:
                        dt_job(it * 2 + 1, 1)
                    if q == 2:
                        zc = z[:, bass.ds(it * TPC, TPC), :]
                        if not last:
                            silu_xs(it + 1)
                        a.activation(zc, zc, ACT.Silu).then_inc(S["a_z"], 1)
                    if q == 3:
                        high(it, 4)
                        if not last:
                            dt_job(it * 2 + 2, 0)
                    if q == NQ - 1 and not last:
                        high(it + 1, 0)
                        for part in range(NA):
                            split_w(it + 1, it * (NQ * NA) + 4 * NA, part)
                    exps(it, 3 if q < 2 else 2)
                exps(it, NU)
                if not last:
                    bt_out(it + 1)

            step(0, True, False)
            with a.Fori(1, NCH - 1) as it:
                step(it, False, False)
            step(NCH - 1, False, True)
            eo_out(NCH - 1, 3)
            eo_out(NCH - 1, 4)
            with a.Fori(0, NCH // 2) as i:
                for h in range(2):
                    c = i * 2 + h
                    a.wait_ge(S["v_total"], c + 1)
                    dst = out[bass.ds(c * TC, TC), :].rearrange("(j p) d -> p j d", p=P)
                    a.dma_start(dst, z[:, bass.ds(c * TPC, TPC), :]).then_inc(d_out[h], 16)
            for h in range(2):
                a.wait_ge(d_out[h], 16 * (NCH // 2))

        @block.vector
        def _(v):
            def statistics(c, h, n):
                v.wait_ge(d_xin[h], n * 16 + 16)
                for j in range(TPC):
                    v.bn_stats(stats[:, j, :], xin[h][:, j, :]).then_inc(S["v_self"], 1)
                v.wait_ge(S["v_self"], c * V0 + TPC)
                settle(v)
                for j in range(TPC):
                    v.bn_aggr(mv[:, j, :], stats[:, j, :]).then_inc(S["v_self"], 1)
                v.wait_ge(S["v_self"], c * V0 + 2 * TPC)
                v.tensor_scalar(mv[:, :, 1], mv[:, :, 1], EPS, None, ALU.add).then_inc(S["var_ready"], 1)

            def normalise(c, h):
                v.wait_ge(S["sd_ready"], c + 1)
                v.reciprocal(rstd[:, :], sd[:, :]).then_inc(S["v_self"], 1)
                v.wait_ge(S["v_self"], c * V0 + 2 * TPC + 1)
                v.wait_ge(S["rows_sent"], c + 1)
                for j in range(TPC):
                    last = v.tensor_scalar(xn[h][:, j, 0:D], xin[h][:, j, :], mv[:, j, 0:1], rstd[:, j:j + 1],
                                           ALU.subtract, ALU.mult)
                last.then_inc(S["xn_ready"], 1)

            def link(c, ins):
                link.n += 1
                ins.then_inc(S["g_self"], 1)
                v.wait_ge(S["g_self"], c * VR + link.n)

            def choose(c, h):
                link.n = 0

                def bc(ap):
                    return ap.unsqueeze(2).to_broadcast([P, TPC, NE])

                v.wait_ge(S["lg_done"], c + 1)
                link(c, v.tensor_copy(lg[:, :, :], ps_l))
                for k, src in enumerate((lg, lg2)):
                    link(c, v.tensor_reduce(top[:, :, k], src[:, :, :], AX, ALU.max))
                    link(c, v.tensor_tensor(eq[:, :, :], src[:, :, :], bc(top[:, :, k]), ALU.is_equal))
                    link(c, v.tensor_tensor(eq[:, :, :], eq[:, :, :], desc[:, :, :], ALU.mult))
                    link(c, v.tensor_reduce(code[:, :, k], eq[:, :, :], AX, ALU.max))
                    link(c, v.tensor_tensor(hot[:, :, k, :], desc[:, :, :], bc(code[:, :, k]), ALU.is_equal))
                    if k == 0:
                        link(c, v.scalar_tensor_tensor(lg2[:, :, :], hot[:, :, 0, :], -3.0e38, lg[:, :, :], ALU.mult, ALU.add))
                v.tensor_tensor(gap[:, bass.ds(c * TPC, TPC)], top[:, :, 1], top[:, :, 0], ALU.subtract)
                v.tensor_tensor(hotb[:, :, :], hot[:, :, 0, :], hot[:, :, 1, :], ALU.add).then_inc(S["hot_ready"], 1)

            def assign(c, h):
                v.tensor_copy(xn[h][:, :, D], tag[:, bass.ds(c * TPC, TPC)])
                v.tensor_copy(xn[h][:, :, D + 1], code[:, :, 0])
                v.wait_ge(S["pos_done"], c + 1)
                link(c, v.tensor_tensor(pos[:, :, :], ps_r, base[:, :].unsqueeze(1).to_broadcast([P, TPC, NE]), ALU.add))
                link(c, v.tensor_tensor(base[:, :], base[:, :], ps_c, ALU.add))
                link(c, v.tensor_tensor(hotpos[:, :, :, :], hot[:, :, :, :], pos[:, :, :].unsqueeze(2).to_broadcast([P, TPC, 2, NE]), ALU.mult))
                link(c, v.tensor_reduce(slot[:, :, :], hotpos[:, :, :, :], AX, ALU.add))
                link(c, v.tensor_scalar(over[:, :, :], slot[:, :, :], float(CAP), float(OUT_OF_BOUNDS), ALU.is_ge, ALU.mult))
                link(c, v.scalar_tensor_tensor(tmp2[:, :, :], slot[:, :, :], float(NE * CAP), over[:, :, :], ALU.add, ALU.add))
                link(c, v.tensor_scalar(kept[:, bass.ds(c * TPC, TPC), :], over[:, :, :], 0.0, None, ALU.is_equal))
                v.scalar_tensor_tensor(sidx[h][:, :].rearrange("p (j k) -> p j k", k=2), code[:, :, :], -float(CAP), tmp2[:, :, :],
                                       ALU.mult, ALU.add).then_inc(S["idx_ready"], 1)
                assert link.n == VR

            def conv(c, taps):
                if 0 in taps:
                    wait(v, "g_u", c * 4)
                    if isinstance(c, int) and c == 0:
                        wait(v, "xc_kept", 1 + 2)
                n = c * 4
                for tap in taps:
                    for m in range(KD):
                        src = xc[:, m, bass.ds(c * TC + tap, TC)]
                        w = par_sb[:, CW + 3 * m + tap:CW + 3 * m + tap + 1]
                        if tap == 0:
                            v.tensor_scalar(xs[:, m, :], src, w, None, ALU.mult).then_inc(S["v_conv_step"], 1)
                        else:
                            v.wait_ge(S["v_conv_step"], n + (2 * (tap - 1) + m + 1))
                            v.scalar_tensor_tensor(xs[:, m, :], src, w, xs[:, m, :], ALU.mult, ALU.add)\
                             .then_inc(S["v_conv_step" if tap == 1 else "v_conv"], 1)

            def b_split(c):
                src = m0[:, 0:TPC * NS].rearrange("p (j n) -> p j n", n=NS)
                hi, mid, lo = (bsplit[:, :, r * NS:(r + 1) * NS] for r in range(3))
                wait(v, "pe_b", c + 1)
                v.tensor_copy(hi, src).then_inc(S["v_bs_step"], 1)
                v.wait_ge(S["v_bs_step"], c * 3 + 1)
                v.tensor_tensor(brest[:, :, :], src, hi, ALU.subtract).then_inc(S["v_bs_step"], 1)
                v.wait_ge(S["v_bs_step"], c * 3 + 2)
                v.tensor_copy(mid, brest[:, :, :]).then_inc(S["v_bs_step"], 1)
                v.wait_ge(S["v_bs_step"], c * 3 + 3)
                v.tensor_tensor(lo, brest[:, :, :], mid, ALU.subtract).then_inc(S["v_bs"], 1)

            def dt_out(J, m):
                wait(v, "a_lg", J + 1)
                v.scalar_tensor_tensor(dt[:, m, :], dt[:, m, :], 1e-5, sp[:, :], ALU.add, ALU.add).then_inc(S["v_dt"], 1)

            def split_w(i, part):
                wait(v, "a_whi", i * (2 * NA) + 2 * (part + 1))
                for k in range(KD):
                    dst, raw, hi = (t[:, :, :].rearrange("p k (g f) -> p k g f", g=2)[:, k, :, part * P:(part + 1) * P]
                                    for t in (w1_lo, w1_raw, w1_hi))
                    last = v.tensor_tensor(dst, raw, hi, ALU.subtract)
                last.then_inc(S["v_wlo"], 1)

            v.sem_inc(S["hot_ready"], 1)
            statistics(0, 0, 0)
            normalise(0, 0)
            statistics(1, 1, 0)
            wait(v, "const_ready", N_CONST)
            with v.Fori(0, 2) as i:
                for h in range(3):
                    c = i * 3 + h
                    choose(c, h)
                    normalise(c + 1, (h + 1) % 3)
                    statistics(c + 2, (h + 2) % 3, i + (h + 2) // 3)
                    assign(c, h)
            choose(NCH - 2, 0)
            normalise(NCH - 1, 1)
            conv(0, (0, 1, 2))
            assign(NCH - 2, 0)
            choose(NCH - 1, 1)
            assign(NCH - 1, 1)
            wait(v, "a_aneg", 1)
            v.tensor_scalar(a_neg[:, :], a_neg[:, :], -1.0, None, ALU.mult).then_inc(S["v_aneg"], 1)
            wait(v, "a_gate", 1)
            v.tensor_scalar(gate[:, :, 0], gap[:, :], 1.0, None, ALU.add).then_inc(S["v_gate"], 1)
            wait(v, "v_gate", 1)
            v.reciprocal(gate[:, :, 0], gate[:, :, 0]).then_inc(S["v_gate"], 1)
            wait(v, "v_gate", 2)
            v.tensor_tensor(gate[:, :, 1], gate[:, :, 0], gap[:, :], ALU.mult).then_inc(S["v_gate"], 1)
            wait(v, "v_gate", 3)
            v.tensor_tensor(gate[:, :, :], gate[:, :, :], kept[:, :, :], ALU.mult).then_inc(S["v_gate"], 1)
            b_split(0)
            for part in range(NA):
                split_w(0, part)
            dt_out(0, 0)
            wait_scatters(v)
            wait(v, "z_done", NCH)
            wait(v, "xc_kept", 1 + NCH)

            def low(it, q):
                b, N = BUF[q], it * NQ + (q + 1)
                wait(v, "a_hi", N)
                v.tensor_tensor(xe_lo[q % 2][:, :, :], m0.rearrange("p (k t) -> p k t", t=QT), xe_hi[q % 2][:, :, :],
                                ALU.subtract).then_inc(S["v_lo"], 1)
                v.tensor_scalar(second[:, :], xe[b][:, :, D + 1], desc[:, 0, bass.ds(it, 1)], float(T),
                                ALU.not_equal, ALU.mult).then_inc(S["v_tag"], 1)
                sb_, uses = buffer(it - 1, q)
                wait(v, d_send[sb_], (uses + 1) * 32)
                wait(v, "v_tag", N)
                v.scalar_tensor_tensor(oidx[q][:, :], xe[b][:, :, D], float(OUT_OF_BOUNDS), second[:, :],
                                       ALU.add, ALU.add).then_inc(S["v_oidx"], 1)

            def drive_unit(it, u):
                if u % NS == 0:
                    wait(v, "g_u", (it * 2 + (u // NS + 1)) * 2)
                wait(v, "pe_bc", it * NU + (u + 1))
                wait(v, "v_scan", it * NU + max(u - 2, min(u - 1, 0)))
                v.tensor_tensor(drive[:, u % 3, :], ps_b[:, u % 2, :], uu[:, u // NS, :], ALU.mult).then_inc(S["v_drive"], 1)

            def units(it, n):
                for _ in range(n):
                    u = units.u
                    units.u += 1
                    if u + 1 < NU:
                        drive_unit(it, u + 1)
                    if u % 4 == 0:
                        wait(v, "g_group", it * 8 + (u // 4 - 1))
                    wait(v, "a_exp", it * NU + (u + 1))
                    wait(v, "v_drive", it * NU + (u + 1))
                    v.tensor_tensor_scan(state[:, (u // 4) % 2, u % 4, :], decay[:, u % 8, :], drive[:, u % 3, :],
                                         carry[:, u:u + 1], ALU.mult, ALU.add).then_inc(S["v_scan"], 1)

            def project_out(c, half):
                wait(v, "pe_op", c * 2 + (half + 1))
                wait(v, "a_z", c + 1)
                zc = z[:, bass.ds(c * TPC + 2 * half, 2), :]
                v.tensor_tensor(zc, zc, m1.rearrange("p (j d) -> p j d", d=D), ALU.mult).then_inc(S["v_op"], 1)

            low(0, 0)

            def step(it, first, last):
                units.u = 0
                drive_unit(it, 0)
                for q in range(NQ):
                    units(it, 1)
                    if q == 1:
                        dt_out(it * 2 + 1, 1)
                    if q == 4 and not last:
                        dt_out(it * 2 + 2, 0)
                    units(it, 1)
                    if q == 3 and not last:
                        b_split(it + 1)
                    if q == 0:
                        low(it, 1)
                    units(it, 1)
                    if q in (1, 2) and not first:
                        project_out(it - 1, q - 1)
                    if q in (1, 2):
                        low(it, q + 1)
                    units(it, 1 if q < 2 else 0)
                    for half in range(2):
                        wait(v, "a_gelu", (it * NQ + q) * 2 + (half + 1))
                        hc = hh[BUF[q]][:, 2 * half:2 * half + 2, :]
                        v.tensor_tensor(hc, hc, ps_h[:, 2 * half:2 * half + 2, 1, :], ALU.mult).then_inc(S["v_h"], 1)
                        if q == 1 and not last:
                            conv(it + 1, (half,))
                        units(it, 1)
                    if q == 1 and not last:
                        conv(it + 1, (2,))
                    if q == 3:
                        low(it, 4)
                    if q == NQ - 1 and not last:
                        low(it + 1, 0)
                        for part in range(NA):
                            split_w(it + 1, part)
                    units(it, 1)
                assert units.u == NU

            step(0, True, False)
            with v.Fori(1, NCH - 1) as it:
                step(it, False, False)
            step(NCH - 1, False, True)
            for half in range(2):
                project_out(NCH - 1, half)

            for c in range(NCH):
                v.wait_ge(d_rows[c % 4], (c // 4) * 32 + 32)
                if c == NCH - 1:
                    v.wait_ge(S["g_x"], NCH + 1)
                for k in range(2):
                    for j in range(TPC):
                        gk = gate[:, c * TPC + j, k:k + 1]
                        zj = z[:, c * TPC + j, :]
                        first_ = rows[c % 4][0][:, j, :]
                        if k == 0:
                            v.scalar_tensor_tensor(first_, first_, gk, zj, ALU.mult, ALU.add).then_inc(S["v_sum"], 1)
                        else:
                            v.wait_ge(S["v_sum"], c * TPC + (j + 1))
                            last = v.scalar_tensor_tensor(zj, rows[c % 4][1][:, j, :], gk, first_, ALU.mult, ALU.add)
                last.then_inc(S["v_total"], 1)

        @block.tensor
        def _(pe):
            mm = nc.tensor.matmul
            wait(pe, "const_ready", N_IDENT)

            def transpose_x(c, h):
                pe.wait_ge(S["xn_ready"], c + 1)
                for k in range(KD):
                    for j in range(TPC):
                        last = nc.tensor.transpose(ps_t[:, k, j * P:(j + 1) * P], xn[h][:, j, k * P:(k + 1) * P], ident[:, :])
                last.then_inc(S["t_done"], 1)

            def chunk(c, h, more):
                pe.wait_ge(S["xnT_ready"], c + 1)
                pe.wait_ge(S["hot_ready"], c + 1)
                for j in range(TPC):
                    for k in range(KD):
                        last = mm(ps_l[:, j, :], xnT[:, k, j * P:(j + 1) * P], wg_sb[:, k, :], start=k == 0, stop=k == KD - 1)
                last.then_inc(S["lg_done"], 1)
                pe.wait_ge(S["xc_kept"], c + 1)
                for m in range(KD):
                    for k in range(KD):
                        last = mm(ps_x[:, m, :], w_in_sb[:, k, m * P:(m + 1) * P], xnT[:, k, :], start=k == 0, stop=k == KD - 1)
                last.then_inc(S["xc_done"], 1)
                pe.wait_ge(S["z_kept"], c + 1)
                for j in range(TPC):
                    for k in range(KD):
                        last = mm(ps_z[:, j, :], xnT[:, k, j * P:(j + 1) * P], w_in_sb[:, k, D:2 * D], start=k == 0, stop=k == KD - 1)
                last.then_inc(S["z_done"], 1)
                if more:
                    transpose_x(c + 1, (h + 1) % 3)
                pe.wait_ge(S["hot_ready"], c + 2)
                for j in range(TPC):
                    mm(ps_r[:, j, :], before[:, :], hotb[:, j, :], start=True, stop=j == 0)
                    for b in range(j):
                        mm(ps_r[:, j, :], onesb[:, :], hotb[:, b, :], start=False, stop=b == j - 1)
                for j in range(TPC):
                    last = mm(ps_c, onesb[:, :], hotb[:, j, :], start=j == 0, stop=j == TPC - 1)
                last.then_inc(S["pos_done"], 1)

            transpose_x(0, 0)
            wait(pe, "d_w", 32)
            wait(pe, "const_ready", N_CONST)
            with pe.Fori(0, 2) as i:
                for h in range(3):
                    chunk(i * 3 + h, h, True)
            chunk(NCH - 2, 0, True)
            chunk(NCH - 1, 1, False)

            def dt_product(J, m, prev):
                wait(pe, *prev)
                mm(m0, w_dtc_sb[0:R, m * P:(m + 1) * P], proj[0:R, :], start=True, stop=True).then_inc(S["pe_dt"], 1)

            def c_product(J, m):
                wait(pe, "a_dt_read", J + 1)
                mm(m0, w_dtc_sb[R:RC, m * P:(m + 1) * P], proj[R:RC, :], start=True, stop=True).then_inc(S["pe_c"], 1)

            def x_dbl(c, prev):
                wait(pe, *prev)
                wait(pe, "a_xs", c + 1)
                for k in range(KD):
                    last = mm(m0[0:RC, :], w_x_sb[:, k, 0:RC], xs[:, k, :], start=k == 0, stop=k == KD - 1)
                last.then_inc(S["pe_xd"], 1)

            def b_product(c):
                wait(pe, "a_proj", c + 1)
                for j in range(TPC):
                    for k in range(KD):
                        last = mm(m0[:, j * NS:(j + 1) * NS], xs[:, k, j * P:(j + 1) * P], w_x_sb[:, k, RC:RC + NS], start=k == 0, stop=k == KD - 1)
                last.then_inc(S["pe_b"], 1)

            def b_transpose(c, prev):
                wait(pe, *prev)
                wait(pe, "v_bs", c + 1)
                settle(pe)
                for j in range(TPC):
                    last = nc.tensor.transpose(m0b[0:3 * NS, j * P:(j + 1) * P], bsplit[:, j, :], identb[:, :])
                last.then_inc(S["pe_bt"], 1)

            wait(pe, "d_w", 80)
            x_dbl(0, ("hot_ready", 1 + NCH))
            b_product(0)
            dt_product(0, 0, ("v_bs", 1))
            c_product(0, 0)
            b_transpose(0, ("a_c", 1))
            wait(pe, "xc_kept", 1 + NCH)
            wait(pe, "z_kept", 1 + NCH)
            wait(pe, "xnT_ready", NCH)
            wait(pe, "idx_ready", NCH)

            def transposes(it, q, prev):
                wait(pe, *prev)
                b, uses = buffer(it, q)
                wait(pe, d_xe[b], (uses + 1) * 16)
                for k in range(KD):
                    for j in range(QT // P):
                        last = nc.tensor.transpose(m0[:, k * QT + j * P:k * QT + (j + 1) * P], xe[b][:, j, k * P:(k + 1) * P], ident[:, :])
                last.then_inc(S["pe_t"], 1)

            def broadcast(it, n=1):
                for _ in range(n):
                    u = broadcast.u
                    if u == NU:
                        return
                    broadcast.u += 1
                    if u == 0:
                        wait(pe, "a_bt", it + 1)
                    wait(pe, "v_drive", it * NU + (u - 1))
                    mm(ps_b[:, u % 2, :], select[:, u % NS, :], bT[:, :], start=True, stop=True).then_inc(S["pe_bc"], 1)

            def first_product(it, q, a):
                if a % 2 == 0:
                    wait(pe, "v_h", (it * NQ + q) * 2 + (a // 2 - 1))
                if a == 0:
                    wait(pe, "v_lo", it * NQ + (q + 1))
                if q == 0:
                    wait(pe, "v_wlo", it * NA + (a + 1))
                for part in range(2):
                    c0 = part * F + a * P
                    n = 0
                    for k in range(KD):
                        for w, xx in ((w1_hi, xe_hi[q % 2]), (w1_hi, xe_lo[q % 2]), (w1_lo, xe_hi[q % 2])):
                            last = mm(ps_h[:, a, part, :], w[:, k, c0:c0 + P], xx[:, k, :], start=n == 0, stop=n == 3 * KD - 1)
                            n += 1
                last.then_inc(S["pe_s1"], 1)

            def second_product(it, q, j):
                if j == 0:
                    wait(pe, "v_h", (it * NQ + q) * 2 + 2)
                    if q == 0:
                        wait(pe, "d_w2", it * 16 + 16)
                for a in range(NA):
                    last = mm(m1[:, j * D:(j + 1) * D], hh[BUF[q]][:, a, j * P:(j + 1) * P], w2_sb[:, a, :], start=a == 0, stop=a == NA - 1)
                if j == QT // P - 1:
                    last.then_inc(S["pe_s2"], 1)

            def out_product(c, half):
                wait(pe, "g_y", c * 2 + 2)
                for j in range(2):
                    t0 = (2 * half + j) * P
                    for m in range(KD):
                        last = mm(m1[:, j * D:(j + 1) * D], yy[:, m, t0:t0 + P], w_out_sb[:, m, :], start=m == 0, stop=m == KD - 1)
                last.then_inc(S["pe_op"], 1)

            transposes(0, 0, ("a_bt", 1))

            def step(it, first, last):
                broadcast.u = 0
                for q in range(NQ):
                    for a in range(NA):
                        first_product(it, q, a)
                        if (q, a) == (0, 0):
                            transposes(it, 1, ("a_bt", it + 1))
                        if (q, a) == (0, 3):
                            dt_product(it * 2 + 1, 1, ("v_lo", it * NQ + 2))
                        if (q, a) == (1, 0):
                            c_product(it * 2 + 1, 1)
                        if (q, a) == (1, 2):
                            transposes(it, 2, ("a_c", it * 2 + 2))
                        if q in (1, 2) and a == 2 and not first:
                            wait(pe, "a_eo", it * NQ + (q - 1))
                            out_product(it - 1, q - 1)
                        if (q, a) == (2, 1):
                            transposes(it, 3, ("v_lo", it * NQ + 3))
                        if (q, a) == (3, 1) and not last:
                            b_product(it + 1)
                        if (q, a) == (3, 3):
                            transposes(it, 4, ("v_lo", it * NQ + 4) if last else ("v_bs", it + 2))
                        if (q, a) == (4, 1) and not last:
                            c_product(it * 2 + 2, 0)
                        broadcast(it)
                    if q == NQ - 1 and not last:
                        transposes(it + 1, 0, ("a_c", it * 2 + 3))
                    broadcast(it)
                    if q in (1, 2) and not first:
                        wait(pe, "v_op", (it - 1) * 2 + q)
                    else:
                        wait(pe, "a_eo", it * NQ + (q - 1))
                    for j in range(QT // P):
                        if q:
                            second_product(it, q - 1, j)
                        elif not first:
                            second_product(it - 1, NQ - 1, j)
                        if q == 2 and j == 1 and not last:
                            x_dbl(it + 1, ("v_lo", it * NQ + 4))
                        if q == 3 and j == 1 and not last:
                            dt_product(it * 2 + 2, 0, ("v_lo", it * NQ + 5))
                        if j == 0 or q < 2:
                            broadcast(it)
                assert broadcast.u == NU
                if not last:
                    b_transpose(it + 1, ("v_lo", it * NQ + (NQ + 1)))

            step(0, True, False)
            with pe.Fori(1, NCH - 1) as it:
                step(it, False, False)
            step(NCH - 1, False, True)
            wait(pe, "a_eo", NCH * NQ - 1)
            for j in range(QT // P):
                second_product(NCH - 1, NQ - 1, j)
            wait(pe, "a_eo", NCH * NQ)
            out_product(NCH - 1, 0)
            wait(pe, "v_op", 2 * NCH - 1)
            out_product(NCH - 1, 1)


N_CONST = 17
N_IDENT = 3
ZERO_DMAS = 12
NZ = NE * CAP * DX // P // ZERO_DMAS
ZERO_OUT_DMAS = 16
NZO = 2 * T * D // P // ZERO_OUT_DMAS
BUF = (0, 1, 0, 1, 2)
V0 = 2 * TPC + 1
VR = 19
G_STEPS = 22


def kernel(**inputs):
    import numpy as np
    import concourse.bacc as bacc
    from concourse.bass_utils import run_bass_kernel_spmd

    def cols(w):
        w = np.asarray(w)
        return np.ascontiguousarray(w.reshape(KD, P, -1).transpose(1, 0, 2))

    i = {k: np.asarray(v) for k, v in inputs.items()}
    w_x = i["L0_attn_W_x"]
    w_x = np.concatenate([w_x[:R], w_x[R + NS:], w_x[R:R + NS]], axis=0)
    par = np.concatenate([cols(i["L0_attn_conv_w"]).reshape(P, -1), cols(i["L0_attn_b_dt"]).reshape(P, -1),
                          cols(i["L0_attn_A_log"]).reshape(P, -1), cols(i["L0_attn_D_param"]).reshape(P, -1)], axis=1)
    arrays = {
        "x": np.ascontiguousarray(i["L0_attn_x"].reshape(T, D)),
        "w_in": cols(i["L0_attn_W_in"].T),
        "w_out": cols(i["L0_attn_W_out"].T),
        "w_x": cols(w_x.T),
        "w_dtc": np.ascontiguousarray(np.concatenate([i["L0_attn_W_dt"].T, i["L0_attn_W_C"].T], axis=0)),
        "wg": cols(i["L0_ffn_Wg"].T),
        "par": np.ascontiguousarray(par),
        "w1": np.ascontiguousarray(i["L0_ffn_W1"].reshape(NE, KD, P, 2 * F).transpose(0, 2, 1, 3).reshape(NE * P, -1)),
        "w2": np.ascontiguousarray(i["L0_ffn_W2"].reshape(NE, NA, P, D).transpose(0, 2, 1, 3).reshape(NE * P, -1)),
    }
    nc = bacc.Bacc("TRN2", target_bir_lowering=False, num_devices=1)
    f32 = mybir.dt.float32
    aps = [nc.dram_tensor(n, a.shape, f32, kind="ExternalInput").ap() for n, a in arrays.items()]
    out = nc.dram_tensor("out", [T, D], f32, kind="ExternalOutput").ap()
    build(nc, *aps, out)
    r = run_bass_kernel_spmd(nc, [arrays], core_ids=[0])
    return r.results[0]["out"].reshape(1, T, D)
```

```python
import concourse.bass as bass
from concourse import mybir
from contextlib import ExitStack

P = 128
T, D, NS, R = 4096, 256, 16, 64
NE, F, CAP = 8, 512, 1280
TC = 512
NCH, TPC, KD = T // TC, TC // P, D // P
QT = 256
NQ, NA = CAP // QT, F // P
NU = KD * NS
EPS = 1e-5
RC = R + NS
CW, CB, CA, CD, CEND = 0, 6, 8, 40, 42
OUT_OF_BOUNDS = 16384
DX = D + 2


def build(nc, x, w_in, w_out, w_x, w_dtc, wg, par, w1, w2, out):
    f32, f32r, bf16 = mybir.dt.float32, mybir.dt.float32r, mybir.dt.bfloat16
    i32, u32 = mybir.dt.int32, mybir.dt.uint32
    ALU, ACT, AX = mybir.AluOpType, mybir.ActivationFunctionType, mybir.AxisListType.X
    table_in = nc.dram_tensor("expert_in", [NE * CAP, DX], f32, kind="Internal").ap()
    table_out = nc.dram_tensor("expert_out", [2 * T, D], f32, kind="Internal").ap()
    ctx = ExitStack()
    with ctx:
        def sb(name, shape, dt=f32):
            return ctx.enter_context(nc.sbuf_tensor(name, shape, dt))

        def sem(name):
            return ctx.enter_context(nc.semaphore(name))

        ident = sb("ident", [P, P])
        identb = sb("identb", [P, P], bf16)
        select = sb("select", [3 * NS, NS, P], bf16)
        desc = sb("desc", [P, TPC, NE])
        w_in_sb = sb("w_in_sb", [P, KD, 2 * D])
        w_out_sb = sb("w_out_sb", [P, KD, D])
        w_x_sb = sb("w_x_sb", [P, KD, R + 2 * NS])
        w_dtc_sb = sb("w_dtc_sb", [RC, D])
        wg_sb = sb("wg_sb", [P, KD, NE])
        par_sb = sb("par_sb", [P, CEND])
        a_neg = sb("a_neg", [P, NU])
        xc = sb("xc", [P, KD, T + 2])
        z = sb("z", [P, T // P, D])
        gate = sb("gate", [P, T // P, 2])
        kept = sb("kept", [P, T // P, 2])
        gap = sb("gap", [P, T // P])
        tag = sb("tag", [P, T // P])
        region = sb("region", [P, 8192])
        xin = [region[:, h * 1024:(h + 1) * 1024].rearrange("p (j d) -> p j d", d=D) for h in range(3)]
        xn = [region[:, 3072 + h * TPC * DX:3072 + (h + 1) * TPC * DX].rearrange("p (j d) -> p j d", d=DX) for h in range(3)]
        xnT = region[:, 6168:7192].rearrange("p (k t) -> p k t", t=TC)
        zeros = z[:, T // P - 7:, :].rearrange("p j d -> p (j d)")[:, 0:NZ]
        decay = region[:, 0:4096].rearrange("p (u t) -> p u t", t=TC)
        state = region[:, 4096:8192].rearrange("p (g u t) -> p g u t", u=4, t=TC)
        cc = sb("cc", [P, KD, TC])
        cc_flat = cc[:, :, :].rearrange("p m t -> p (m t)")
        used = [0]

        def small(shape, dt=f32):
            n = 1
            for d in shape[1:]:
                n *= d
            words = n // 2 if dt == bf16 else n
            ap = cc_flat[:, used[0]:used[0] + words]
            used[0] += words
            assert used[0] <= KD * TC
            if dt == bf16:
                ap = ap.bitcast(bf16)
            if len(shape) == 3:
                return ap.rearrange("p (a b) -> p a b", b=shape[2])
            if len(shape) == 4:
                return ap.rearrange("p (a b c) -> p a b c", b=shape[2], c=shape[3])
            return ap

        before = small([P, P], bf16)
        onesb = small([P, P], bf16)
        stats = small([P, TPC, 6])
        mv = small([P, TPC, 2])
        sd = small([P, TPC])
        rstd = small([P, TPC])
        lg = small([P, TPC, NE])
        lg2 = small([P, TPC, NE])
        eq = small([P, TPC, NE])
        top = small([P, TPC, 2])
        code = small([P, TPC, 2])
        hot = small([P, TPC, 2, NE])
        hotb = small([P, TPC, NE], bf16)
        base = sb("base", [P, NE])
        pos = small([P, TPC, NE])
        hotpos = small([P, TPC, 2, NE])
        slot = small([P, TPC, 2])
        over = small([P, TPC, 2])
        tmp2 = small([P, TPC, 2])
        sidx = [sb(f"sidx{h}", [P, TPC * 2], i32) for h in range(3)]
        xs = sb("xs", [P, KD, TC])
        proj = sb("proj", [RC, TC])
        dt = sb("dt", [P, KD, TC])
        uu = sb("uu", [P, KD, TC])
        dx = sb("dx", [P, KD, TC])
        yy = sb("yy", [P, KD, TC])
        sp = sb("sp", [P, TC])
        bsplit = sb("bsplit", [P, TPC, 3 * NS], bf16)
        brest = sb("brest", [P, TPC, NS])
        bT = sb("bT", [3 * NS, TC], bf16)
        drive = sb("drive", [P, 3, TC])
        carry = sb("carry", [P, NU])
        hsum = sb("hsum", [P, TC])
        xres = w_in_sb[:, :, :].rearrange("p k (j d) -> p (k j) d", d=D)
        w1_raw = sb("w1_raw", [P, KD, 2 * F])
        w1_hi = sb("w1_hi", [P, KD, 2 * F], f32r)
        w1_lo = sb("w1_lo", [P, KD, 2 * F], f32r)
        w2_sb = sb("w2_sb", [P, NA, D])
        xe = [sb(f"xe{b}", [P, QT // P, DX]) for b in range(3)]
        xe_hi = [sb(f"xe_hi{b}", [P, KD, QT], f32r) for b in range(2)]
        xe_lo = [sb(f"xe_lo{b}", [P, KD, QT], f32r) for b in range(2)]
        hh = [sb(f"hh{b}", [P, NA, QT]) for b in range(3)]
        eo = [sb(f"eo{b}", [P, QT // P, D]) for b in range(3)]
        rows = [[t.rearrange("p (j d) -> p j d", d=D) for t in pair] for pair in
                ([w1_raw[:, k, :] for k in range(2)], [hh[b][:, :, :].rearrange("p a t -> p (a t)") for b in range(2)],
                 [region[:, k * 1024:(k + 1) * 1024] for k in range(2)], [region[:, k * 1024:(k + 1) * 1024] for k in range(2, 4)])]
        second = sb("second", [P, QT // P])
        oidx_sb = sb("oidx", [P, NQ, QT // P], i32)
        oidx = [oidx_sb[:, q, :] for q in range(NQ)]

        ps = ctx.enter_context(nc.psum_tensor("ps", [P, 8, 512], f32))
        ps_t = ps[:, 0:2, :]
        ps_x = ps[:, 2:4, :]
        ps_z = ps[:, 4:6, :].rearrange("p b (j d) -> p (b j) d", d=D)
        ps_l = ps[:, 6, 0:TPC * NE].rearrange("p (j e) -> p j e", e=NE)
        ps_r = ps[:, 7, 0:TPC * NE].rearrange("p (j e) -> p j e", e=NE)
        ps_c = ps[:, 7, TPC * NE:(TPC + 1) * NE]
        ps_h = ps[:, 0:4, :].rearrange("p a (g t) -> p a g t", t=QT)
        ps_b = ps[:, 4:6, :]
        m0 = ps[:, 6, :]
        m1 = ps[:, 7, :]
        m0b = m0.bitcast(bf16)

        names = """settled v_tag const_ready d_w d_par zero_done zero_out
            var_ready sd_ready xn_ready t_done xnT_ready xc_done xc_kept lg_done hot_ready z_done z_kept
            pos_done idx_ready rows_sent v_self a_self g_self
            pe_t pe_bc pe_s1 pe_s2 pe_dt pe_c pe_xd pe_b pe_bt pe_op
            a_hi a_whi a_dt_read a_abs a_ex a_lg a_c a_proj a_bt a_exp a_gelu a_eo a_xs a_z a_aneg a_gate
            v_lo v_wlo v_dt v_drive v_scan v_conv v_conv_step v_bs v_bs_step v_h v_op v_aneg v_oidx v_total v_gate
            g_u g_group g_step g_y g_y_step g_x
            d_raw d_w2 d_xr d_out a_scaled g_sum""".split()
        S = {n: sem(n) for n in names}
        d_xin = [sem(f"d_xin{h}") for h in range(3)]
        d_scatter = [sem(f"d_scatter{h}") for h in range(3)]
        d_xe = [sem(f"d_xe{b}") for b in range(3)]
        d_send = [sem(f"d_send{b}") for b in range(3)]
        d_rows = [sem(f"d_rows{b}") for b in range(4)]

        def wait(eng, name, value):
            if isinstance(value, int) and value <= 0:
                return
            eng.wait_ge(S[name] if isinstance(name, str) else name, value)

        def buffer(it, q):
            return BUF[q], it * BUF.count(BUF[q]) + BUF[:q].count(BUF[q])

        def wait_scatters(eng):
            for h in range(3):
                eng.wait_ge(d_scatter[h], 32 * TPC * len(range(h, NCH, 3)))

        def settle(eng):
            eng.sem_inc(S["settled"], 1)

        def x_rows(c, n=TPC):
            return x[bass.ds(c * TC, n * P), :].rearrange("(j p) d -> p j d", p=P)

        block = ctx.enter_context(nc.Block())

        @block.sync
        def _(sp_):
            e = sp_

            def load_x(c, h):
                e.dma_start(xin[h], x_rows(c)).then_inc(d_xin[h], 16)

            def load_w1(i):
                e.dma_start(w1_raw[:, :, :], w1[bass.ds(i * P, P), :].rearrange("p (k f) -> p k f", k=KD)).then_inc(S["d_raw"], 16)

            def load_w2(i):
                e.dma_start(w2_sb[:, :, :], w2[bass.ds(i * P, P), :].rearrange("p (a d) -> p a d", a=NA)).then_inc(S["d_w2"], 16)

            def load_xe(i, q):
                src = table_in[bass.ds(i * CAP + q * QT, QT), :].rearrange("(j p) d -> p j d", p=P)
                e.dma_start(xe[BUF[q]][:, :, :], src).then_inc(d_xe[BUF[q]], 16)

            def load(name, tile, src):
                e.dma_start(tile, src).then_inc(S[name], 16)

            tin = table_in.rearrange("(p r) d -> p (r d)", p=P)
            tout = table_out.rearrange("(p r) d -> p (r d)", p=P)

            def zero_in(ns):
                for n in ns:
                    e.dma_start(tin[:, n * NZ:(n + 1) * NZ], zeros).then_inc(S["zero_done"], 16)

            def zero_out(ns):
                for n in ns:
                    e.dma_start(tout[:, n * NZO:(n + 1) * NZO], zeros[:, 0:NZO]).then_inc(S["zero_out"], 16)

            load_x(0, 0)
            load("d_w", w_in_sb[:, :, :], w_in)
            load("d_w", wg_sb[:, :, :], wg)
            load_x(1, 1)
            load("d_par", par_sb[:, :], par)
            wait(e, "const_ready", 1)
            zero_in(range(0, 6))
            load_x(2, 2)
            zero_in(range(6, ZERO_DMAS))
            for c in range(3, NCH):
                e.wait_ge(S["xn_ready"], c - 2)
                load_x(c, c % 3)
                if c == 4:
                    load("d_w", w_x_sb[:, :, :], w_x)
                    load("d_w", w_dtc_sb[:, :], w_dtc)
                    load("d_w", w_out_sb[:, :, :], w_out)
                    load_w1(0)
                zero_out({5: range(0, 6), 6: range(6, 11), 7: range(11, ZERO_OUT_DMAS)}.get(c, ()))

            load_w2(0)
            wait_scatters(e)
            load_xe(0, 0)
            load_xe(0, 1)

            def next_xe(it, q):
                wait(e, "pe_t", it * NQ + (q - 1))
                wait(e, "v_oidx", it * NQ + (q - 1))
                load_xe(it + q // NQ, q % NQ)

            def step(it, first, last):
                if not first:
                    wait(e, "pe_s2", it * NQ)
                    load_w2(it)
                    wait(e, "g_x", it)
                    e.dma_start(xres, x_rows(it - 1)).then_inc(S["d_xr"], 16)
                next_xe(it, 2)
                if not last:
                    wait(e, "v_wlo", it * NA + NA)
                    load_w1(it + 1)
                for q in range(3, NQ if last else NQ + 2):
                    next_xe(it, q)

            step(0, True, False)
            with e.Fori(1, NCH - 1) as it:
                step(it, False, False)
            step(NCH - 1, False, True)
            wait(e, "g_x", NCH)
            e.dma_start(xres, x_rows(NCH - 1)).then_inc(S["d_xr"], 16)
            for b in range(3):
                e.wait_ge(d_send[b], 32 * NE * BUF.count(b))
            wait(e, "v_wlo", NCH * NA)
            for c in range(NCH):
                if c == 1:
                    wait(e, "pe_s2", NCH * NQ - 1)
                if c == 2:
                    wait(e, "v_scan", NCH * NU)
                if c >= 4:
                    e.wait_ge(S["v_total"], c - 3)
                for k in range(2):
                    src = table_out[c * TC + k * T:(c + 1) * TC + k * T, :].rearrange("(j p) d -> p j d", p=P)
                    e.dma_start(rows[c % 4][k], src).then_inc(d_rows[c % 4], 16)

        @block.gpsimd
        def _(g):
            cnt = [0]

            def inc(ins):
                cnt[0] += 1
                ins.then_inc(S["const_ready"], 1)

            inc(g.memset(zeros, 0.0))
            inc(g.memset(ident[:, :], 0.0))
            wait(g, "const_ready", cnt[0])
            inc(g.affine_select(out=ident[:, :], in_=ident[:, :], compare_op=ALU.not_equal, fill=1.0,
                                base=0, pattern=[[-1, P]], channel_multiplier=1))
            assert cnt[0] == N_IDENT
            inc(g.memset(before[:, :], 1.0))
            inc(g.memset(onesb[:, :], 1.0))
            inc(g.memset(select[:, :, :], 0.0))
            inc(g.memset(xc[:, :, 0:1], 0.0))
            inc(g.memset(xc[:, :, T + 1:T + 2], 0.0))
            inc(g.memset(carry[:, :], 0.0))
            inc(g.memset(base[:, :], 0.0))
            inc(g.iota(tag[:, :], pattern=[[P, T // P]], base=-OUT_OF_BOUNDS, channel_multiplier=1,
                       allow_small_or_imprecise_dtypes=True))
            inc(g.iota(desc[:, :, :], pattern=[[0, TPC], [-1, NE]], base=NE, channel_multiplier=0,
                       allow_small_or_imprecise_dtypes=True))
            wait(g, "const_ready", cnt[0])
            inc(g.affine_select(out=before[:, :], in_=before[:, :], compare_op=ALU.is_gt, fill=0.0,
                                base=0, pattern=[[1, P]], channel_multiplier=-1))
            for r in range(3):
                wait(g, "const_ready", cnt[0])
                inc(g.affine_select(out=select[:, :, :], in_=select[:, :, :], compare_op=ALU.not_equal, fill=1.0,
                                    base=-NS * r, pattern=[[-1, NS], [0, P]], channel_multiplier=1))
            wait(g, "const_ready", cnt[0])
            inc(g.tensor_copy(identb[:, :], ident[:, :]))
            assert cnt[0] == N_CONST
            g.sem_inc(S["g_x"], 1)
            g.sem_inc(S["rows_sent"], 3)
            wait(g, "zero_done", 16 * ZERO_DMAS)

            def scatter(c, h):
                g.wait_ge(S["idx_ready"], c + 1)
                settle(g)
                for n in range(2 * TPC):
                    g.indirect_dma_start(table_in, bass.IndirectOffsetOnAxis(ap=sidx[h][:, n:n + 1].bitcast(u32), axis=0),
                                         xn[h][:, n // 2, :], None, bounds_check=NE * CAP - 1,
                                         oob_is_err=False).then_inc(d_scatter[h], 16)

            with g.Fori(0, 2) as i:
                for h in range(3):
                    scatter(i * 3 + h, h)
                    for done in ((), (0,), (1, 2))[h]:
                        g.wait_ge(d_scatter[done], (i + 1) * (32 * TPC))
                        g.sem_inc(S["rows_sent"], 1)
            scatter(6, 0)
            scatter(7, 1)

            def drive_job(J, m):
                wait(g, "v_dt", J + 1)
                wait(g, "g_y", J - 1)
                g.tensor_tensor(uu[:, m, :], dt[:, m, :], xs[:, m, :], ALU.mult).then_inc(S["g_u"], 1)
                g.tensor_scalar(dx[:, m, :], xs[:, m, :], par_sb[:, CD + m:CD + m + 1], 0.0, ALU.mult, ALU.add).then_inc(S["g_u"], 1)

            def group(it, G, between=None):
                b, m = G % 2, G // 4
                wait(g, "v_scan", it * NU + (4 * G + 4))
                settle(g)
                g.tensor_copy(carry[:, 4 * G:4 * G + 4], state[:, b, :, TC - 1]).then_inc(S["g_step"], 1)
                wait(g, "g_step", it * G_STEPS + group.n + 1)
                g.tensor_tensor(state[:, b, 0:2, :], state[:, b, 0:2, :], state[:, b, 2:4, :], ALU.add).then_inc(S["g_step"], 1)
                if between is not None:
                    send(it, between)
                wait(g, "g_step", it * G_STEPS + group.n + 2)
                if G % 4 == 0:
                    wait(g, "g_y", it * 2 + m)
                    g.tensor_tensor(hsum[:, :], state[:, b, 0, :], state[:, b, 1, :], ALU.add).then_inc(S["g_group"], 1)
                    group.n += 2
                else:
                    g.tensor_tensor(state[:, b, 0, :], state[:, b, 0, :], state[:, b, 1, :], ALU.add).then_inc(S["g_step"], 1)
                    wait(g, "g_step", it * G_STEPS + group.n + 3)
                    wait(g, "g_group", it * 8 + G)
                    g.tensor_tensor(hsum[:, :], hsum[:, :], state[:, b, 0, :], ALU.add).then_inc(S["g_group"], 1)
                    group.n += 3

            def y_job(it, m):
                J = it * 2 + m
                wait(g, "g_group", it * 8 + 4 * (m + 1))
                wait(g, "a_c", J + 1)
                wait(g, "pe_op", it * 2)
                g.tensor_tensor(hsum[:, :], hsum[:, :], cc[:, m, :], ALU.mult).then_inc(S["g_y_step"], 1)
                wait(g, "g_y_step", J + 1)
                g.tensor_tensor(yy[:, m, :], hsum[:, :], dx[:, m, :], ALU.add).then_inc(S["g_y"], 1)

            def add_x(c):
                wait(g, "v_op", c * 2 + 2)
                wait(g, "d_xr", (c + 1) * 16)
                zc = z[:, bass.ds(c * TPC, TPC), :]
                g.tensor_tensor(zc, zc, xres, ALU.add).then_inc(S["g_x"], 1)

            def send(it, q):
                b, before_ = buffer(it, q)
                wait(g, "a_eo", it * NQ + (q + 1))
                wait(g, "v_oidx", it * NQ + (q + 1))
                settle(g)
                for j in range(QT // P):
                    g.indirect_dma_start(table_out, bass.IndirectOffsetOnAxis(ap=oidx[q][:, j:j + 1].bitcast(u32), axis=0),
                                         eo[b][:, j, :], None, bounds_check=2 * T - 1, oob_is_err=False).then_inc(d_send[b], 16)

            drive_job(0, 0)

            def step(it, first, last):
                group.n = 0
                if not first:
                    send(it - 1, 3)
                group(it, 0)
                drive_job(it * 2 + 1, 1)
                group(it, 1)
                if not first:
                    send(it - 1, 4)
                group(it, 2)
                if not first:
                    add_x(it - 1)
                if first:
                    wait(g, "zero_out", 16 * ZERO_OUT_DMAS)
                send(it, 0)
                group(it, 3)
                y_job(it, 0)
                group(it, 4)
                send(it, 1)
                group(it, 5)
                if not last:
                    drive_job(it * 2 + 2, 0)
                send(it, 2)
                group(it, 6)
                if last:
                    send(it, 3)
                group(it, 7, 4 if last else None)
                y_job(it, 1)
                assert group.n == G_STEPS

            step(0, True, False)
            with g.Fori(1, NCH - 1) as it:
                step(it, False, False)
            step(NCH - 1, False, True)
            for c in range(NCH):
                if c == NCH // 2:
                    add_x(NCH - 1)
                    wait(g, "g_x", NCH + 1)
                g.wait_ge(S["a_scaled"], c + 1)
                first_ = rows[c % 4][0]
                g.tensor_tensor(first_, first_, z[:, c * TPC:(c + 1) * TPC, :], ALU.add).then_inc(S["g_sum"], 1)

        @block.scalar
        def _(a):
            a.sem_inc(S["xc_kept"], 1)
            a.sem_inc(S["z_kept"], 1)
            wait(a, "d_par", 16)
            a.activation(a_neg[:, :], par_sb[:, CA:CA + NU], ACT.Exp).then_inc(S["a_aneg"], 1)

            def deviation(c):
                a.wait_ge(S["var_ready"], c + 1)
                a.activation(sd[:, :], mv[:, :, 1], ACT.Sqrt).then_inc(S["sd_ready"], 1)

            def keep_xnT(c):
                a.wait_ge(S["t_done"], c + 1)
                a.activation(xnT, ps_t, ACT.Copy).then_inc(S["xnT_ready"], 1)

            def keep_xc(c):
                a.wait_ge(S["xc_done"], c + 1)
                a.activation(xc[:, :, bass.ds(c * TC + 1, TC)], ps_x, ACT.Copy).then_inc(S["xc_kept"], 1)

            def keep_z(c):
                a.wait_ge(S["z_done"], c + 1)
                a.activation(z[:, bass.ds(c * TPC, TPC), :], ps_z, ACT.Copy).then_inc(S["z_kept"], 1)

            def keep(c):
                keep_xc(c)
                keep_z(c)
                if isinstance(c, int) and c == NCH - 1:
                    return
                keep_xnT(c + 1)
                if isinstance(c, int) and c == NCH - 2:
                    return
                deviation(c + 2)

            def split_w(i, q4, part):
                if q4 is not None:
                    wait(a, "pe_s1", q4 + part + 1)
                if part == 0:
                    wait(a, "d_raw", i * 16 + 16)
                dst = w1_hi[:, :, :].rearrange("p k (g f) -> p k g f", g=2)[:, :, :, part * P:(part + 1) * P]
                src = w1_raw[:, :, :].rearrange("p k (g f) -> p k g f", g=2)[:, :, :, part * P:(part + 1) * P]
                for k in range(KD):
                    a.activation(dst[:, k], src[:, k], ACT.Copy).then_inc(S["a_whi"], 1)

            def dt_job(J, m):
                b = par_sb[:, CB + m:CB + m + 1]
                wait(a, "pe_dt", J + 1)
                wait(a, "v_dt", J)
                wait(a, "g_u", 2 * J - 2)
                a.activation(sp[:, :], m0, ACT.Abs, bias=b).then_inc(S["a_abs"], 1)
                a.activation(dt[:, m, :], m0, ACT.Relu, bias=b).then_inc(S["a_dt_read"], 1)

            def dt_log(J):
                wait(a, "a_abs", J + 1)
                a.activation(sp[:, :], sp[:, :], ACT.Exp, scale=-1.0).then_inc(S["a_ex"], 1)
                wait(a, "a_ex", J + 1)
                a.activation(sp[:, :], sp[:, :], ACT.Ln, bias=1.0).then_inc(S["a_lg"], 1)

            def c_job(J, m):
                wait(a, "pe_c", J + 1)
                wait(a, "g_y", J - 1)
                a.activation(cc[:, m, :], m0, ACT.Copy).then_inc(S["a_c"], 1)

            def silu_xs(c):
                wait(a, "v_conv", c * 2 + 2)
                a.activation(xs[:, :, :], xs[:, :, :], ACT.Silu).then_inc(S["a_xs"], 1)

            def proj_out(c):
                wait(a, "pe_xd", c + 1)
                a.activation(proj[:, :], m0[0:RC, :], ACT.Copy).then_inc(S["a_proj"], 1)

            def bt_out(c):
                wait(a, "pe_bt", c + 1)
                a.activation(bT[:, :], m0b[0:3 * NS, 0:TC], ACT.Copy).then_inc(S["a_bt"], 1)

            deviation(0)
            keep_xnT(0)
            deviation(1)
            with a.Fori(0, 2) as i:
                for h in range(3):
                    keep(i * 3 + h)
            wait(a, "zero_done", 16 * ZERO_DMAS)
            wait(a, "zero_out", 16 * ZERO_OUT_DMAS)
            for part in range(2):
                split_w(0, None, part)
            keep(NCH - 2)
            for part in range(2, NA):
                split_w(0, None, part)
            silu_xs(0)
            keep(NCH - 1)

            proj_out(0)
            a.wait_ge(S["hot_ready"], 1 + NCH)
            a.activation(gap[:, :], gap[:, :], ACT.Exp).then_inc(S["a_gate"], 1)
            dt_job(0, 0)
            dt_log(0)
            wait(a, "idx_ready", NCH)
            c_job(0, 0)
            bt_out(0)
            wait_scatters(a)

            def high(it, q):
                wait(a, "pe_t", it * NQ + (q + 1))
                a.activation(xe_hi[q % 2][:, :, :], m0.rearrange("p (k t) -> p k t", t=QT), ACT.Copy).then_inc(S["a_hi"], 1)

            def decays(it, u):
                if u % NS == 0:
                    wait(a, "v_dt", it * 2 + (u // NS + 1))
                wait(a, "v_scan", it * NU + (u - 7))
                a.activation(decay[:, u % 8, :], dt[:, u // NS, :], ACT.Exp, scale=a_neg[:, u:u + 1]).then_inc(S["a_exp"], 1)

            def gelu(it, q, half):
                if half == 0:
                    wait(a, "pe_s2", it * NQ + (-2, -1, 1, 2, 0)[q])
                wait(a, "pe_s1", (it * NQ + q) * NA + (2 * half + 2))
                a.activation(hh[BUF[q]][:, 2 * half:2 * half + 2, :], ps_h[:, 2 * half:2 * half + 2, 0, :], ACT.Gelu).then_inc(S["a_gelu"], 1)

            def silu_z(it):
                zc = z[:, bass.ds(it * TPC, TPC), :]
                a.activation(zc, zc, ACT.Silu).then_inc(S["a_z"], 1)

            def eo_out(it, q):
                b, uses = buffer(it, q)
                wait(a, "pe_s2", it * NQ + (q + 1))
                wait(a, d_send[b], uses * 32)
                a.activation(eo[b][:, :, :], m1.rearrange("p (j d) -> p j d", d=D), ACT.Copy).then_inc(S["a_eo"], 1)

            high(0, 0)

            def step(it, first, last):
                decays(it, 0)
                decays(it, 1)
                decays(it, 2)
                decays(it, 3)
                decays(it, 4)
                decays(it, 5)
                high(it, 1)
                if not first:
                    eo_out(it - 1, 3)
                decays(it, 6)
                gelu(it, 0, 0)
                gelu(it, 0, 1)
                dt_job(it * 2 + 1, 1)
                dt_log(it * 2 + 1)
                decays(it, 7)
                decays(it, 8)
                decays(it, 9)
                if not first:
                    eo_out(it - 1, 4)
                decays(it, 10)
                decays(it, 11)
                c_job(it * 2 + 1, 1)
                decays(it, 12)
                high(it, 2)
                decays(it, 13)
                gelu(it, 1, 0)
                gelu(it, 1, 1)
                eo_out(it, 0)
                decays(it, 14)
                decays(it, 15)
                decays(it, 16)
                decays(it, 17)
                decays(it, 18)
                decays(it, 19)
                decays(it, 20)
                high(it, 3)
                gelu(it, 2, 0)
                gelu(it, 2, 1)
                if not last:
                    silu_xs(it + 1)
                silu_z(it)
                eo_out(it, 1)
                decays(it, 21)
                decays(it, 22)
                if not last:
                    proj_out(it + 1)
                decays(it, 23)
                decays(it, 24)
                decays(it, 25)
                decays(it, 26)
                gelu(it, 3, 0)
                gelu(it, 3, 1)
                high(it, 4)
                if not last:
                    dt_job(it * 2 + 2, 0)
                    dt_log(it * 2 + 2)
                decays(it, 27)
                decays(it, 28)
                decays(it, 29)
                decays(it, 30)
                eo_out(it, 2)
                if not last:
                    c_job(it * 2 + 2, 0)
                decays(it, 31)
                gelu(it, 4, 0)
                gelu(it, 4, 1)
                if not last:
                    split_w(it + 1, it * (NQ * NA) + 4 * NA, 0)
                    split_w(it + 1, it * (NQ * NA) + 4 * NA, 1)
                    high(it + 1, 0)
                    split_w(it + 1, it * (NQ * NA) + 4 * NA, 2)
                    split_w(it + 1, it * (NQ * NA) + 4 * NA, 3)
                    bt_out(it + 1)

            step(0, True, False)
            with a.Fori(1, NCH - 1) as it:
                step(it, False, False)
            step(NCH - 1, False, True)
            eo_out(NCH - 1, 3)
            eo_out(NCH - 1, 4)

            def store(c):
                a.wait_ge(S["v_total"], c + 1)
                dst = out[c * TC:(c + 1) * TC, :].rearrange("(j p) d -> p j d", p=P)
                a.dma_start(dst, z[:, c * TPC:(c + 1) * TPC, :]).then_inc(S["d_out"], 16)

            for c in range(NCH):
                a.wait_ge(d_rows[c % 4], (c // 4) * 32 + 32)
                for j in range(TPC):
                    last = a.activation(rows[c % 4][0][:, j, :], rows[c % 4][0][:, j, :], ACT.Copy, scale=gate[:, c * TPC + j, 0:1])
                last.then_inc(S["a_scaled"], 1)
                if c >= 2:
                    store(c - 2)
            for c in range(NCH - 2, NCH):
                store(c)
            a.wait_ge(S["d_out"], 16 * NCH)

        @block.vector
        def _(v):
            def statistics(c, h, n):
                v.wait_ge(d_xin[h], n * 16 + 16)
                for j in range(TPC):
                    v.bn_stats(stats[:, j, :], xin[h][:, j, :]).then_inc(S["v_self"], 1)
                v.wait_ge(S["v_self"], c * V0 + TPC)
                settle(v)
                for j in range(TPC):
                    v.bn_aggr(mv[:, j, :], stats[:, j, :]).then_inc(S["v_self"], 1)
                v.wait_ge(S["v_self"], c * V0 + 2 * TPC)
                v.tensor_scalar(mv[:, :, 1], mv[:, :, 1], EPS, None, ALU.add).then_inc(S["var_ready"], 1)

            def normalise(c, h):
                v.wait_ge(S["sd_ready"], c + 1)
                v.reciprocal(rstd[:, :], sd[:, :]).then_inc(S["v_self"], 1)
                v.wait_ge(S["v_self"], c * V0 + 2 * TPC + 1)
                v.wait_ge(S["rows_sent"], c + 1)
                for j in range(TPC):
                    last = v.tensor_scalar(xn[h][:, j, 0:D], xin[h][:, j, :], mv[:, j, 0:1], rstd[:, j:j + 1],
                                           ALU.subtract, ALU.mult)
                last.then_inc(S["xn_ready"], 1)

            def link(c, ins):
                link.n += 1
                ins.then_inc(S["g_self"], 1)
                v.wait_ge(S["g_self"], c * VR + link.n)

            def choose(c, h):
                link.n = 0

                def bc(ap):
                    return ap.unsqueeze(2).to_broadcast([P, TPC, NE])

                v.wait_ge(S["lg_done"], c + 1)
                link(c, v.tensor_copy(lg[:, :, :], ps_l))
                for k, src in enumerate((lg, lg2)):
                    link(c, v.tensor_reduce(top[:, :, k], src[:, :, :], AX, ALU.max))
                    link(c, v.tensor_tensor(eq[:, :, :], src[:, :, :], bc(top[:, :, k]), ALU.is_equal))
                    link(c, v.tensor_tensor(eq[:, :, :], eq[:, :, :], desc[:, :, :], ALU.mult))
                    link(c, v.tensor_reduce(code[:, :, k], eq[:, :, :], AX, ALU.max))
                    link(c, v.tensor_tensor(hot[:, :, k, :], desc[:, :, :], bc(code[:, :, k]), ALU.is_equal))
                    if k == 0:
                        link(c, v.scalar_tensor_tensor(lg2[:, :, :], hot[:, :, 0, :], -3.0e38, lg[:, :, :], ALU.mult, ALU.add))
                v.tensor_tensor(gap[:, bass.ds(c * TPC, TPC)], top[:, :, 1], top[:, :, 0], ALU.subtract)
                v.tensor_tensor(hotb[:, :, :], hot[:, :, 0, :], hot[:, :, 1, :], ALU.add).then_inc(S["hot_ready"], 1)

            def assign(c, h):
                v.tensor_copy(xn[h][:, :, D], tag[:, bass.ds(c * TPC, TPC)])
                v.tensor_copy(xn[h][:, :, D + 1], code[:, :, 0])
                v.wait_ge(S["pos_done"], c + 1)
                link(c, v.tensor_tensor(pos[:, :, :], ps_r, base[:, :].unsqueeze(1).to_broadcast([P, TPC, NE]), ALU.add))
                link(c, v.tensor_tensor(base[:, :], base[:, :], ps_c, ALU.add))
                link(c, v.tensor_tensor(hotpos[:, :, :, :], hot[:, :, :, :], pos[:, :, :].unsqueeze(2).to_broadcast([P, TPC, 2, NE]), ALU.mult))
                link(c, v.tensor_reduce(slot[:, :, :], hotpos[:, :, :, :], AX, ALU.add))
                link(c, v.tensor_scalar(over[:, :, :], slot[:, :, :], float(CAP), float(OUT_OF_BOUNDS), ALU.is_ge, ALU.mult))
                link(c, v.scalar_tensor_tensor(tmp2[:, :, :], slot[:, :, :], float(NE * CAP), over[:, :, :], ALU.add, ALU.add))
                link(c, v.tensor_scalar(kept[:, bass.ds(c * TPC, TPC), :], over[:, :, :], 0.0, None, ALU.is_equal))
                v.scalar_tensor_tensor(sidx[h][:, :].rearrange("p (j k) -> p j k", k=2), code[:, :, :], -float(CAP), tmp2[:, :, :],
                                       ALU.mult, ALU.add).then_inc(S["idx_ready"], 1)
                assert link.n == VR

            def conv(c, taps):
                if 0 in taps:
                    wait(v, "g_u", c * 4)
                    if isinstance(c, int) and c == 0:
                        wait(v, "xc_kept", 1 + 2)
                n = c * 4
                for tap in taps:
                    for m in range(KD):
                        src = xc[:, m, bass.ds(c * TC + tap, TC)]
                        w = par_sb[:, CW + 3 * m + tap:CW + 3 * m + tap + 1]
                        if tap == 0:
                            v.tensor_scalar(xs[:, m, :], src, w, None, ALU.mult).then_inc(S["v_conv_step"], 1)
                        else:
                            v.wait_ge(S["v_conv_step"], n + (2 * (tap - 1) + m + 1))
                            v.scalar_tensor_tensor(xs[:, m, :], src, w, xs[:, m, :], ALU.mult, ALU.add)\
                             .then_inc(S["v_conv_step" if tap == 1 else "v_conv"], 1)

            def b_split(c):
                src = m0[:, 0:TPC * NS].rearrange("p (j n) -> p j n", n=NS)
                hi, mid, lo = (bsplit[:, :, r * NS:(r + 1) * NS] for r in range(3))
                wait(v, "pe_b", c + 1)
                v.tensor_copy(hi, src).then_inc(S["v_bs_step"], 1)
                v.wait_ge(S["v_bs_step"], c * 3 + 1)
                v.tensor_tensor(brest[:, :, :], src, hi, ALU.subtract).then_inc(S["v_bs_step"], 1)
                v.wait_ge(S["v_bs_step"], c * 3 + 2)
                v.tensor_copy(mid, brest[:, :, :]).then_inc(S["v_bs_step"], 1)
                v.wait_ge(S["v_bs_step"], c * 3 + 3)
                v.tensor_tensor(lo, brest[:, :, :], mid, ALU.subtract).then_inc(S["v_bs"], 1)

            def dt_out(J, m):
                wait(v, "a_lg", J + 1)
                v.scalar_tensor_tensor(dt[:, m, :], dt[:, m, :], 1e-5, sp[:, :], ALU.add, ALU.add).then_inc(S["v_dt"], 1)

            def split_w(i, part):
                wait(v, "a_whi", i * (2 * NA) + 2 * (part + 1))
                for k in range(KD):
                    dst, raw, hi = (t[:, :, :].rearrange("p k (g f) -> p k g f", g=2)[:, k, :, part * P:(part + 1) * P]
                                    for t in (w1_lo, w1_raw, w1_hi))
                    last = v.tensor_tensor(dst, raw, hi, ALU.subtract)
                last.then_inc(S["v_wlo"], 1)

            v.sem_inc(S["hot_ready"], 1)
            statistics(0, 0, 0)
            normalise(0, 0)
            statistics(1, 1, 0)
            wait(v, "const_ready", N_CONST)
            with v.Fori(0, 2) as i:
                for h in range(3):
                    c = i * 3 + h
                    choose(c, h)
                    normalise(c + 1, (h + 1) % 3)
                    statistics(c + 2, (h + 2) % 3, i + (h + 2) // 3)
                    assign(c, h)
            choose(NCH - 2, 0)
            normalise(NCH - 1, 1)
            conv(0, (0, 1, 2))
            assign(NCH - 2, 0)
            choose(NCH - 1, 1)
            assign(NCH - 1, 1)
            b_split(0)
            for part in range(NA):
                split_w(0, part)
            wait(v, "a_aneg", 1)
            v.tensor_scalar(a_neg[:, :], a_neg[:, :], -1.0, None, ALU.mult).then_inc(S["v_aneg"], 1)
            dt_out(0, 0)
            wait(v, "a_gate", 1)
            v.tensor_scalar(gate[:, :, 0], gap[:, :], 1.0, None, ALU.add).then_inc(S["v_gate"], 1)
            wait(v, "v_gate", 1)
            v.reciprocal(gate[:, :, 0], gate[:, :, 0]).then_inc(S["v_gate"], 1)
            wait(v, "v_gate", 2)
            v.tensor_tensor(gate[:, :, 1], gate[:, :, 0], gap[:, :], ALU.mult).then_inc(S["v_gate"], 1)
            wait(v, "v_gate", 3)
            v.tensor_tensor(gate[:, :, :], gate[:, :, :], kept[:, :, :], ALU.mult).then_inc(S["v_gate"], 1)
            wait_scatters(v)
            wait(v, "z_done", NCH)
            wait(v, "xc_kept", 1 + NCH)

            def low(it, q):
                b, N = BUF[q], it * NQ + (q + 1)
                wait(v, "a_hi", N)
                v.tensor_tensor(xe_lo[q % 2][:, :, :], m0.rearrange("p (k t) -> p k t", t=QT), xe_hi[q % 2][:, :, :],
                                ALU.subtract).then_inc(S["v_lo"], 1)
                v.tensor_scalar(second[:, :], xe[b][:, :, D + 1], desc[:, 0, bass.ds(it, 1)], float(T),
                                ALU.not_equal, ALU.mult).then_inc(S["v_tag"], 1)
                sb_, uses = buffer(it - 1, q)
                wait(v, d_send[sb_], (uses + 1) * 32)
                wait(v, "v_tag", N)
                v.scalar_tensor_tensor(oidx[q][:, :], xe[b][:, :, D], float(OUT_OF_BOUNDS), second[:, :],
                                       ALU.add, ALU.add).then_inc(S["v_oidx"], 1)

            def drive_unit(it, u):
                if u % NS == 0:
                    wait(v, "g_u", (it * 2 + (u // NS + 1)) * 2)
                wait(v, "pe_bc", it * NU + (u + 1))
                wait(v, "v_scan", it * NU + max(u - 2, min(u - 1, 0)))
                v.tensor_tensor(drive[:, u % 3, :], ps_b[:, u % 2, :], uu[:, u // NS, :], ALU.mult).then_inc(S["v_drive"], 1)

            def scan(it, u):
                if u % 4 == 0:
                    wait(v, "g_group", it * 8 + (u // 4 - 1))
                wait(v, "a_exp", it * NU + (u + 1))
                wait(v, "v_drive", it * NU + (u + 1))
                v.tensor_tensor_scan(state[:, (u // 4) % 2, u % 4, :], decay[:, u % 8, :], drive[:, u % 3, :],
                                     carry[:, u:u + 1], ALU.mult, ALU.add).then_inc(S["v_scan"], 1)

            def gated(it, q, half):
                wait(v, "a_gelu", (it * NQ + q) * 2 + (half + 1))
                hc = hh[BUF[q]][:, 2 * half:2 * half + 2, :]
                v.tensor_tensor(hc, hc, ps_h[:, 2 * half:2 * half + 2, 1, :], ALU.mult).then_inc(S["v_h"], 1)

            def project_out(c, half, bank=m1):
                wait(v, "pe_op", c * 2 + (half + 1))
                wait(v, "a_z", c + 1)
                zc = z[:, bass.ds(c * TPC + 2 * half, 2), :]
                v.tensor_tensor(zc, zc, bank.rearrange("p (j d) -> p j d", d=D), ALU.mult).then_inc(S["v_op"], 1)

            low(0, 0)

            def step(it, first, last):
                drive_unit(it, 0)
                drive_unit(it, 1)
                scan(it, 0)
                drive_unit(it, 2)
                scan(it, 1)
                low(it, 1)
                drive_unit(it, 3)
                scan(it, 2)
                gated(it, 0, 0)
                drive_unit(it, 4)
                scan(it, 3)
                drive_unit(it, 5)
                scan(it, 4)
                gated(it, 0, 1)
                scan(it, 5)
                drive_unit(it, 6)
                drive_unit(it, 7)
                scan(it, 6)
                drive_unit(it, 8)
                scan(it, 7)
                dt_out(it * 2 + 1, 1)
                drive_unit(it, 9)
                scan(it, 8)
                drive_unit(it, 10)
                scan(it, 9)
                if not first:
                    project_out(it - 1, 0)
                drive_unit(it, 11)
                low(it, 2)
                scan(it, 10)
                gated(it, 1, 0)
                drive_unit(it, 12)
                if not last:
                    conv(it + 1, (0,))
                scan(it, 11)
                gated(it, 1, 1)
                if not last:
                    conv(it + 1, (1,))
                drive_unit(it, 13)
                scan(it, 12)
                if not last:
                    conv(it + 1, (2,))
                drive_unit(it, 14)
                scan(it, 13)
                drive_unit(it, 15)
                scan(it, 14)
                if not first:
                    project_out(it - 1, 1)
                gated(it, 2, 0)
                drive_unit(it, 16)
                scan(it, 15)
                drive_unit(it, 17)
                scan(it, 16)
                low(it, 3)
                drive_unit(it, 18)
                scan(it, 17)
                gated(it, 2, 1)
                drive_unit(it, 19)
                scan(it, 18)
                drive_unit(it, 20)
                scan(it, 19)
                drive_unit(it, 21)
                scan(it, 20)
                drive_unit(it, 22)
                scan(it, 21)
                if not last:
                    b_split(it + 1)
                drive_unit(it, 23)
                low(it, 4)
                gated(it, 3, 0)
                scan(it, 22)
                gated(it, 3, 1)
                drive_unit(it, 24)
                scan(it, 23)
                drive_unit(it, 25)
                scan(it, 24)
                drive_unit(it, 26)
                scan(it, 25)
                if not last:
                    dt_out(it * 2 + 2, 0)
                drive_unit(it, 27)
                scan(it, 26)
                drive_unit(it, 28)
                scan(it, 27)
                scan(it, 28)
                drive_unit(it, 29)
                scan(it, 29)
                gated(it, 4, 0)
                drive_unit(it, 30)
                gated(it, 4, 1)
                drive_unit(it, 31)
                scan(it, 30)
                if not last:
                    low(it + 1, 0)
                    split_w(it + 1, 0)
                scan(it, 31)
                if not last:
                    split_w(it + 1, 1)
                    split_w(it + 1, 2)
                    split_w(it + 1, 3)

            step(0, True, False)
            with v.Fori(1, NCH - 1) as it:
                step(it, False, False)
            step(NCH - 1, False, True)
            for half in range(2):
                project_out(NCH - 1, half, m1 if half == 0 else ps[:, 0, :])

            for c in range(NCH):
                v.wait_ge(S["g_sum"], c + 1)
                for j in range(TPC):
                    last = v.scalar_tensor_tensor(z[:, c * TPC + j, :], rows[c % 4][1][:, j, :], gate[:, c * TPC + j, 1:2],
                                                  rows[c % 4][0][:, j, :], ALU.mult, ALU.add)
                last.then_inc(S["v_total"], 1)

        @block.tensor
        def _(pe):
            mm = nc.tensor.matmul
            wait(pe, "const_ready", N_IDENT)

            def transpose_x(c, h):
                pe.wait_ge(S["xn_ready"], c + 1)
                for k in range(KD):
                    for j in range(TPC):
                        last = nc.tensor.transpose(ps_t[:, k, j * P:(j + 1) * P], xn[h][:, j, k * P:(k + 1) * P], ident[:, :])
                last.then_inc(S["t_done"], 1)

            def chunk(c, h, more):
                pe.wait_ge(S["xnT_ready"], c + 1)
                pe.wait_ge(S["hot_ready"], c + 1)
                for j in range(TPC):
                    for k in range(KD):
                        last = mm(ps_l[:, j, :], xnT[:, k, j * P:(j + 1) * P], wg_sb[:, k, :], start=k == 0, stop=k == KD - 1)
                last.then_inc(S["lg_done"], 1)
                pe.wait_ge(S["xc_kept"], c + 1)
                for m in range(KD):
                    for k in range(KD):
                        last = mm(ps_x[:, m, :], w_in_sb[:, k, m * P:(m + 1) * P], xnT[:, k, :], start=k == 0, stop=k == KD - 1)
                last.then_inc(S["xc_done"], 1)
                pe.wait_ge(S["z_kept"], c + 1)
                for j in range(TPC):
                    for k in range(KD):
                        last = mm(ps_z[:, j, :], xnT[:, k, j * P:(j + 1) * P], w_in_sb[:, k, D:2 * D], start=k == 0, stop=k == KD - 1)
                last.then_inc(S["z_done"], 1)
                if more:
                    transpose_x(c + 1, (h + 1) % 3)
                pe.wait_ge(S["hot_ready"], c + 2)
                for j in range(TPC):
                    mm(ps_r[:, j, :], before[:, :], hotb[:, j, :], start=True, stop=j == 0)
                    for b in range(j):
                        mm(ps_r[:, j, :], onesb[:, :], hotb[:, b, :], start=False, stop=b == j - 1)
                for j in range(TPC):
                    last = mm(ps_c, onesb[:, :], hotb[:, j, :], start=j == 0, stop=j == TPC - 1)
                last.then_inc(S["pos_done"], 1)

            transpose_x(0, 0)
            wait(pe, "d_w", 32)
            wait(pe, "const_ready", N_CONST)
            with pe.Fori(0, 2) as i:
                for h in range(3):
                    chunk(i * 3 + h, h, True)
            chunk(NCH - 2, 0, True)
            chunk(NCH - 1, 1, False)

            def dt_product(J, m, prev):
                wait(pe, *prev)
                mm(m0, w_dtc_sb[0:R, m * P:(m + 1) * P], proj[0:R, :], start=True, stop=True).then_inc(S["pe_dt"], 1)

            def c_product(J, m):
                wait(pe, "a_dt_read", J + 1)
                mm(m0, w_dtc_sb[R:RC, m * P:(m + 1) * P], proj[R:RC, :], start=True, stop=True).then_inc(S["pe_c"], 1)

            def x_dbl(c, prev):
                wait(pe, *prev)
                wait(pe, "a_xs", c + 1)
                for k in range(KD):
                    last = mm(m0[0:RC, :], w_x_sb[:, k, 0:RC], xs[:, k, :], start=k == 0, stop=k == KD - 1)
                last.then_inc(S["pe_xd"], 1)

            def b_product(c):
                wait(pe, "a_proj", c + 1)
                for j in range(TPC):
                    for k in range(KD):
                        last = mm(m0[:, j * NS:(j + 1) * NS], xs[:, k, j * P:(j + 1) * P], w_x_sb[:, k, RC:RC + NS], start=k == 0, stop=k == KD - 1)
                last.then_inc(S["pe_b"], 1)

            def b_transpose(c, prev):
                wait(pe, *prev)
                wait(pe, "v_bs", c + 1)
                settle(pe)
                for j in range(TPC):
                    last = nc.tensor.transpose(m0b[0:3 * NS, j * P:(j + 1) * P], bsplit[:, j, :], identb[:, :])
                last.then_inc(S["pe_bt"], 1)

            wait(pe, "d_w", 80)
            x_dbl(0, ("hot_ready", 1 + NCH))
            b_product(0)
            dt_product(0, 0, ("v_bs", 1))
            c_product(0, 0)
            b_transpose(0, ("a_c", 1))
            wait(pe, "xc_kept", 1 + NCH)
            wait(pe, "z_kept", 1 + NCH)
            wait(pe, "xnT_ready", NCH)
            wait(pe, "idx_ready", NCH)

            def transposes(it, q, prev):
                wait(pe, *prev)
                b, uses = buffer(it, q)
                wait(pe, d_xe[b], (uses + 1) * 16)
                for k in range(KD):
                    for j in range(QT // P):
                        last = nc.tensor.transpose(m0[:, k * QT + j * P:k * QT + (j + 1) * P], xe[b][:, j, k * P:(k + 1) * P], ident[:, :])
                last.then_inc(S["pe_t"], 1)

            def broadcast(it, u):
                if u == 0:
                    wait(pe, "a_bt", it + 1)
                wait(pe, "v_drive", it * NU + (u - 1))
                mm(ps_b[:, u % 2, :], select[:, u % NS, :], bT[:, :], start=True, stop=True).then_inc(S["pe_bc"], 1)

            def first_product(it, q, a):
                if a % 2 == 0:
                    wait(pe, "v_h", (it * NQ + q) * 2 + (a // 2 - 1))
                if a == 0:
                    wait(pe, "v_lo", it * NQ + (q + 1))
                if q == 0:
                    wait(pe, "v_wlo", it * NA + (a + 1))
                for part in range(2):
                    c0 = part * F + a * P
                    n = 0
                    for k in range(KD):
                        for w, xx in ((w1_hi, xe_hi[q % 2]), (w1_hi, xe_lo[q % 2]), (w1_lo, xe_hi[q % 2])):
                            last = mm(ps_h[:, a, part, :], w[:, k, c0:c0 + P], xx[:, k, :], start=n == 0, stop=n == 3 * KD - 1)
                            n += 1
                last.then_inc(S["pe_s1"], 1)

            def second_product(it, q, j):
                if j == 0:
                    wait(pe, "v_h", (it * NQ + q) * 2 + 2)
                    if q == 0:
                        wait(pe, "d_w2", it * 16 + 16)
                for a in range(NA):
                    last = mm(m1[:, j * D:(j + 1) * D], hh[BUF[q]][:, a, j * P:(j + 1) * P], w2_sb[:, a, :], start=a == 0, stop=a == NA - 1)
                if j == QT // P - 1:
                    last.then_inc(S["pe_s2"], 1)

            def out_product(c, half, bank=m1):
                wait(pe, "g_y", c * 2 + 2)
                for j in range(2):
                    t0 = (2 * half + j) * P
                    for m in range(KD):
                        last = mm(bank[:, j * D:(j + 1) * D], yy[:, m, t0:t0 + P], w_out_sb[:, m, :], start=m == 0, stop=m == KD - 1)
                last.then_inc(S["pe_op"], 1)

            transposes(0, 0, ("a_bt", 1))

            def step(it, first, last):
                first_product(it, 0, 0)
                transposes(it, 1, ("a_bt", it + 1))
                broadcast(it, 0)
                first_product(it, 0, 1)
                broadcast(it, 1)
                first_product(it, 0, 2)
                broadcast(it, 2)
                first_product(it, 0, 3)
                broadcast(it, 3)
                dt_product(it * 2 + 1, 1, ("v_lo", it * NQ + 2))
                broadcast(it, 4)
                if not first:
                    wait(pe, "a_eo", it * NQ - 1)
                    second_product(it - 1, NQ - 1, 0)
                broadcast(it, 5)
                if not first:
                    second_product(it - 1, NQ - 1, 1)
                first_product(it, 1, 0)
                broadcast(it, 6)
                broadcast(it, 7)
                c_product(it * 2 + 1, 1)
                first_product(it, 1, 1)
                broadcast(it, 8)
                first_product(it, 1, 2)
                broadcast(it, 9)
                first_product(it, 1, 3)
                broadcast(it, 10)
                if not first:
                    wait(pe, "a_eo", it * NQ + 0)
                    out_product(it - 1, 0)
                transposes(it, 2, ("a_c", it * 2 + 2))
                broadcast(it, 11)
                wait(pe, *(("v_op", it * 2 + -1) if not first else ("a_eo", it * NQ + 0)))
                second_product(it, 0, 0)
                broadcast(it, 12)
                second_product(it, 0, 1)
                broadcast(it, 13)
                first_product(it, 2, 0)
                broadcast(it, 14)
                first_product(it, 2, 1)
                broadcast(it, 15)
                first_product(it, 2, 2)
                transposes(it, 3, ("v_lo", it * NQ + 3))
                if not first:
                    wait(pe, "a_eo", it * NQ + 1)
                    out_product(it - 1, 1)
                broadcast(it, 16)
                first_product(it, 2, 3)
                broadcast(it, 17)
                broadcast(it, 18)
                wait(pe, *(("v_op", it * 2 + 0) if not first else ("a_eo", it * NQ + 1)))
                second_product(it, 1, 0)
                second_product(it, 1, 1)
                if not last:
                    x_dbl(it + 1, ("v_lo", it * NQ + 4))
                first_product(it, 3, 0)
                broadcast(it, 19)
                broadcast(it, 20)
                first_product(it, 3, 1)
                broadcast(it, 21)
                first_product(it, 3, 2)
                wait(pe, "a_eo", it * NQ + 2)
                second_product(it, 2, 0)
                broadcast(it, 22)
                if not last:
                    b_product(it + 1)
                broadcast(it, 23)
                first_product(it, 3, 3)
                broadcast(it, 24)
                transposes(it, 4, ("v_bs", it + 2) if not last else ("v_lo", it * NQ + 4))
                broadcast(it, 25)
                second_product(it, 2, 1)
                if not last:
                    dt_product(it * 2 + 2, 0, ("v_lo", it * NQ + 5))
                first_product(it, 4, 0)
                if not last:
                    c_product(it * 2 + 2, 0)
                broadcast(it, 26)
                first_product(it, 4, 1)
                broadcast(it, 27)
                first_product(it, 4, 2)
                broadcast(it, 28)
                first_product(it, 4, 3)
                broadcast(it, 29)
                if not last:
                    transposes(it + 1, 0, ("a_c", it * 2 + 3))
                broadcast(it, 30)
                wait(pe, "a_eo", it * NQ + 3)
                second_product(it, 3, 0)
                broadcast(it, 31)
                second_product(it, 3, 1)
                if not last:
                    b_transpose(it + 1, ("v_lo", it * NQ + 6))

            step(0, True, False)
            with pe.Fori(1, NCH - 1) as it:
                step(it, False, False)
            step(NCH - 1, False, True)
            wait(pe, "a_eo", NCH * NQ - 1)
            for j in range(QT // P):
                second_product(NCH - 1, NQ - 1, j)
            wait(pe, "a_eo", NCH * NQ)
            out_product(NCH - 1, 0)
            out_product(NCH - 1, 1, ps[:, 0, :])


N_CONST = 17
N_IDENT = 3
ZERO_DMAS = 12
NZ = NE * CAP * DX // P // ZERO_DMAS
ZERO_OUT_DMAS = 16
NZO = 2 * T * D // P // ZERO_OUT_DMAS
BUF = (0, 1, 0, 1, 2)
V0 = 2 * TPC + 1
VR = 19
G_STEPS = 22


def kernel(**inputs):
    import numpy as np
    import concourse.bacc as bacc
    from concourse.bass_utils import run_bass_kernel_spmd

    def cols(w):
        w = np.asarray(w)
        return np.ascontiguousarray(w.reshape(KD, P, -1).transpose(1, 0, 2))

    i = {k: np.asarray(v) for k, v in inputs.items()}
    w_x = i["L0_attn_W_x"]
    w_x = np.concatenate([w_x[:R], w_x[R + NS:], w_x[R:R + NS]], axis=0)
    par = np.concatenate([cols(i["L0_attn_conv_w"]).reshape(P, -1), cols(i["L0_attn_b_dt"]).reshape(P, -1),
                          cols(i["L0_attn_A_log"]).reshape(P, -1), cols(i["L0_attn_D_param"]).reshape(P, -1)], axis=1)
    arrays = {
        "x": np.ascontiguousarray(i["L0_attn_x"].reshape(T, D)),
        "w_in": cols(i["L0_attn_W_in"].T),
        "w_out": cols(i["L0_attn_W_out"].T),
        "w_x": cols(w_x.T),
        "w_dtc": np.ascontiguousarray(np.concatenate([i["L0_attn_W_dt"].T, i["L0_attn_W_C"].T], axis=0)),
        "wg": cols(i["L0_ffn_Wg"].T),
        "par": np.ascontiguousarray(par),
        "w1": np.ascontiguousarray(i["L0_ffn_W1"].reshape(NE, KD, P, 2 * F).transpose(0, 2, 1, 3).reshape(NE * P, -1)),
        "w2": np.ascontiguousarray(i["L0_ffn_W2"].reshape(NE, NA, P, D).transpose(0, 2, 1, 3).reshape(NE * P, -1)),
    }
    nc = bacc.Bacc("TRN2", target_bir_lowering=False, num_devices=1)
    f32 = mybir.dt.float32
    aps = [nc.dram_tensor(n, a.shape, f32, kind="ExternalInput").ap() for n, a in arrays.items()]
    out = nc.dram_tensor("out", [T, D], f32, kind="ExternalOutput").ap()
    build(nc, *aps, out)
    r = run_bass_kernel_spmd(nc, [arrays], core_ids=[0])
    return r.results[0]["out"].reshape(1, T, D)
```
